# Optimizing a Trainium2 kernel written in Bass

```python
import numpy as np
import jax
import jax.numpy as jnp

def _softmax(x, axis=-1):
    return jax.nn.softmax(x, axis=axis)

def _gelu(x):
    return jax.nn.gelu(x, approximate=True)

def _silu(x):
    return jax.nn.silu(x)

def _sigmoid(x):
    return jax.nn.sigmoid(x)

def _layernorm(x, axis=-1, eps=1e-05):
    m = jnp.mean(x, axis=axis, keepdims=True)
    v = jnp.var(x, axis=axis, keepdims=True)
    return (x - m) / jnp.sqrt(v + eps)

def _scatter_add(tgt, idx, src, axis=0):
    return tgt.at[idx].add(src)

def _segment_sum(src, seg, n):
    return jax.ops.segment_sum(src, seg, n)
kernel_name = 'mk_macaron_d1_jaxref_r8_c78214'

def setup_inputs(seed: int=0):
    np.random.seed(seed)
    _w = jnp.asarray

    def _L0_attn_setup():
        import jax, jax.numpy as jnp
        import numpy as np
        import math
        DIM = 128
        NUM_HEADS = 8
        HEAD_DIM = DIM // NUM_HEADS // 2
        DEPTH = 6
        LAMBDA_INIT = 0.8 - 0.6 * math.exp(-0.3 * DEPTH)
        EPS = 1e-05
        key = jax.random.key(seed)
        ks = jax.random.split(key, 10)
        B, S = (2, 256)
        x = jax.random.normal(ks[0], (B, S, DIM), dtype=jnp.float32)
        sc = DIM ** (-0.5)
        Wq = jax.random.normal(ks[1], (DIM, DIM), dtype=jnp.float32) * sc
        Wk = jax.random.normal(ks[2], (DIM, DIM), dtype=jnp.float32) * sc
        Wv = jax.random.normal(ks[3], (DIM, DIM), dtype=jnp.float32) * sc
        Wo = jax.random.normal(ks[4], (DIM, DIM), dtype=jnp.float32) * sc
        lq1 = jax.random.normal(ks[5], (HEAD_DIM,), dtype=jnp.float32) * 0.1
        lk1 = jax.random.normal(ks[6], (HEAD_DIM,), dtype=jnp.float32) * 0.1
        lq2 = jax.random.normal(ks[7], (HEAD_DIM,), dtype=jnp.float32) * 0.1
        lk2 = jax.random.normal(ks[8], (HEAD_DIM,), dtype=jnp.float32) * 0.1
        return {'x': x, 'Wq': Wq, 'Wk': Wk, 'Wv': Wv, 'Wo': Wo, 'lq1': lq1, 'lk1': lk1, 'lq2': lq2, 'lk2': lk2}
    _L0_attn_in = _L0_attn_setup()

    def _L0_ffn_setup():
        import jax, jax.numpy as jnp
        import numpy as np
        E = 8
        K = 2
        D = 128
        F = 512
        EPS = 1e-05

        def _layernorm(h, g, b):
            mu = h.mean(axis=-1, keepdims=True)
            var = ((h - mu) ** 2).mean(axis=-1, keepdims=True)
            return (h - mu) * jax.lax.rsqrt(var + EPS) * g[:, None, :] + b[:, None, :]
        key = jax.random.key(seed)
        ks = jax.random.split(key, 8)
        B, S = (2, 256)
        x = jax.random.normal(ks[0], (B, S, D), dtype=jnp.float32)
        Wr = jax.random.normal(ks[1], (D, E), dtype=jnp.float32) / np.sqrt(D)
        br = jnp.zeros((E,), dtype=jnp.float32)
        W1 = jax.random.normal(ks[2], (E, D, F), dtype=jnp.float32) / np.sqrt(D)
        b1 = jnp.zeros((E, F), dtype=jnp.float32)
        g1 = jnp.ones((E, F), dtype=jnp.float32)
        be1 = jnp.zeros((E, F), dtype=jnp.float32)
        W2 = jax.random.normal(ks[3], (E, F, D), dtype=jnp.float32) / np.sqrt(F)
        b2 = jnp.zeros((E, D), dtype=jnp.float32)
        g2 = jnp.ones((E, D), dtype=jnp.float32)
        be2 = jnp.zeros((E, D), dtype=jnp.float32)
        return {'x': x, 'Wr': Wr, 'br': br, 'W1': W1, 'b1': b1, 'g1': g1, 'be1': be1, 'W2': W2, 'b2': b2, 'g2': g2, 'be2': be2}
    _L0_ffn_in = _L0_ffn_setup()
    _d = {'L0_attn_x': _L0_attn_in['x'], 'L0_attn_Wq': _L0_attn_in['Wq'], 'L0_attn_Wk': _L0_attn_in['Wk'], 'L0_attn_Wv': _L0_attn_in['Wv'], 'L0_attn_Wo': _L0_attn_in['Wo'], 'L0_attn_lq1': _L0_attn_in['lq1'], 'L0_attn_lk1': _L0_attn_in['lk1'], 'L0_attn_lq2': _L0_attn_in['lq2'], 'L0_attn_lk2': _L0_attn_in['lk2'], 'L0_ffn_Wr': _L0_ffn_in['Wr'], 'L0_ffn_br': _L0_ffn_in['br'], 'L0_ffn_W1': _L0_ffn_in['W1'], 'L0_ffn_b1': _L0_ffn_in['b1'], 'L0_ffn_g1': _L0_ffn_in['g1'], 'L0_ffn_be1': _L0_ffn_in['be1'], 'L0_ffn_W2': _L0_ffn_in['W2'], 'L0_ffn_b2': _L0_ffn_in['b2'], 'L0_ffn_g2': _L0_ffn_in['g2'], 'L0_ffn_be2': _L0_ffn_in['be2']}
    _x0 = _d['L0_attn_x']
    _d['L0_attn_x'] = jax.random.normal(jax.random.fold_in(jax.random.key(seed), 1), (8, 256, 128), dtype=_x0.dtype)
    del _x0
    return _d

def reference(L0_attn_x, L0_attn_Wq, L0_attn_Wk, L0_attn_Wv, L0_attn_Wo, L0_attn_lq1, L0_attn_lk1, L0_attn_lq2, L0_attn_lk2, L0_ffn_Wr, L0_ffn_br, L0_ffn_W1, L0_ffn_b1, L0_ffn_g1, L0_ffn_be1, L0_ffn_W2, L0_ffn_b2, L0_ffn_g2, L0_ffn_be2):

    def _L0_attn_ref(x, Wq, Wk, Wv, Wo, lq1, lk1, lq2, lk2):
        import jax, jax.numpy as jnp
        import numpy as np
        import math
        DIM = 128
        NUM_HEADS = 8
        HEAD_DIM = DIM // NUM_HEADS // 2
        DEPTH = 6
        LAMBDA_INIT = 0.8 - 0.6 * math.exp(-0.3 * DEPTH)
        EPS = 1e-05
        B, S, D = x.shape
        H, hd = (NUM_HEADS, HEAD_DIM)
        scaling = hd ** (-0.5)
        q = (x @ Wq.T).reshape(B, S, 2 * H, hd).transpose(0, 2, 1, 3) * scaling
        k = (x @ Wk.T).reshape(B, S, 2 * H, hd).transpose(0, 2, 1, 3)
        v = (x @ Wv.T).reshape(B, S, H, 2 * hd).transpose(0, 2, 1, 3)
        scores = jnp.einsum('bhqd,bhkd->bhqk', q, k)
        scores = jnp.nan_to_num(scores)
        causal = jnp.triu(jnp.full((S, S), -jnp.inf, dtype=scores.dtype), 1)
        attn = jax.nn.softmax(scores + causal, axis=-1)
        lam1 = jnp.exp(jnp.sum(lq1 * lk1))
        lam2 = jnp.exp(jnp.sum(lq2 * lk2))
        lam = lam1 - lam2 + LAMBDA_INIT
        attn = attn.reshape(B, H, 2, S, S)
        w = attn[:, :, 0] - lam * attn[:, :, 1]
        o = jnp.einsum('bhqk,bhkd->bhqd', w, v)
        o = o * jax.lax.rsqrt(jnp.mean(o * o, axis=-1, keepdims=True) + EPS)
        o = o * (1.0 - LAMBDA_INIT)
        o = o.transpose(0, 2, 1, 3).reshape(B, S, H * 2 * hd)
        return o @ Wo.T

    def _L0_ffn_ref(x, Wr, br, W1, b1, g1, be1, W2, b2, g2, be2):
        import jax, jax.numpy as jnp
        import numpy as np
        E = 8
        K = 2
        D = 128
        F = 512
        EPS = 1e-05

        def _layernorm(h, g, b):
            mu = h.mean(axis=-1, keepdims=True)
            var = ((h - mu) ** 2).mean(axis=-1, keepdims=True)
            return (h - mu) * jax.lax.rsqrt(var + EPS) * g[:, None, :] + b[:, None, :]
        B, S, _ = x.shape
        xt = x.reshape(-1, D)
        logits = xt @ Wr + br
        p = jax.nn.softmax(logits, axis=-1)
        probs, idx = jax.lax.top_k(p, K)
        probs = probs / probs.sum(axis=-1, keepdims=True)
        h = jnp.einsum('td,edf->etf', xt, W1) + b1[:, None, :]
        h = _layernorm(jax.nn.relu(h), g1, be1)
        y = jnp.einsum('etf,efd->etd', h, W2) + b2[:, None, :]
        y = _layernorm(jax.nn.relu(y), g2, be2)
        gate = (jax.nn.one_hot(idx, E, dtype=x.dtype) * probs[..., None]).sum(axis=1)
        out = jnp.einsum('te,etd->td', gate, y)
        return out.reshape(B, S, D)
    x = L0_attn_x
    x = x + 0.5 * _L0_ffn_ref(_layernorm(x, axis=-1), L0_ffn_Wr, L0_ffn_br, L0_ffn_W1, L0_ffn_b1, L0_ffn_g1, L0_ffn_be1, L0_ffn_W2, L0_ffn_b2, L0_ffn_g2, L0_ffn_be2)
    x = x + _L0_attn_ref(_layernorm(x, axis=-1), L0_attn_Wq, L0_attn_Wk, L0_attn_Wv, L0_attn_Wo, L0_attn_lq1, L0_attn_lk1, L0_attn_lq2, L0_attn_lk2)
    x = x + 0.5 * _L0_ffn_ref(_layernorm(x, axis=-1), L0_ffn_Wr, L0_ffn_br, L0_ffn_W1, L0_ffn_b1, L0_ffn_g1, L0_ffn_be1, L0_ffn_W2, L0_ffn_b2, L0_ffn_g2, L0_ffn_be2)
    return x

_drawn_inputs = setup_inputs


def setup_inputs(seed=0):
    import zlib

    import numpy as np

    out = dict(_drawn_inputs(seed))
    spreads = {'L0_ffn_br': (0.0, 0.1),
     'L0_ffn_b1': (0.0, 0.1),
     'L0_ffn_g1': (1.0, 0.2),
     'L0_ffn_be1': (0.0, 0.1),
     'L0_ffn_b2': (0.0, 0.1),
     'L0_ffn_g2': (1.0, 0.2),
     'L0_ffn_be2': (0.0, 0.1)}
    factors = {'L0_attn_lq1': 3.871, 'L0_attn_lk1': 3.058}
    for name, (base, spread) in spreads.items():
        noise = np.random.default_rng([zlib.crc32(name.encode()), seed]).standard_normal(out[name].shape)
        drawn = base * np.exp(spread * noise) if base else spread * noise
        out[name] = jnp.asarray(drawn.astype(out[name].dtype))
    for name, factor in factors.items():
        out[name] = (out[name] * factor).astype(out[name].dtype)
    return out
```

```python
from contextlib import ExitStack
import math

import concourse.bass as bass
from concourse import mybir

F32 = mybir.dt.float32
BF16 = mybir.dt.bfloat16
I32 = mybir.dt.int32
U32 = mybir.dt.uint32
ALU = mybir.AluOpType
ACT = mybir.ActivationFunctionType
X = mybir.AxisListType.X

P = 128
BATCH, SEQ, DIM = 8, 256, 128
TOK = BATCH * SEQ
TT = TOK // P
NE, TOPK, FF = 8, 2, 512
FC = FF // P
SLOT_TILES = TOPK * TOK // P + NE - 1
EPS = 1e-5
BIG = 3.0e38


HEADS, HD, SUB = 8, 8, 16
VD = DIM // HEADS
SLOTS, MAXSLOT = 8, 6
LAMBDA_INIT = 0.8 - 0.6 * math.exp(-0.3 * 6)
GUARD = 2.0 ** 60
ATT_STEPS = 26


class Steps:

    def __init__(self, eng, sem):
        self.eng, self.sem, self.n = eng, sem, 0

    def __call__(self, ins):
        ins.then_inc(self.sem, 1)
        self.n += 1
        self.eng.wait_ge(self.sem, self.n)


class LoopSteps:

    def __init__(self, eng, sem):
        self.eng, self.sem, self.base, self.n = eng, sem, 0, 0

    def start(self, base):
        self.base, self.n = base, 0

    def __call__(self, ins):
        ins.then_inc(self.sem, 1)
        self.n += 1
        self.eng.wait_ge(self.sem, self.base + self.n)


def build(nc, x, Wq, Wk, Wv, Wo, lq1, lk1, lq2, lk2, Wr, br, W1, b1, g1, be1, W2, b2, g2, be2, out, stages=("f1", "at", "f2")):
    with ExitStack() as ctx:
        def sb(name, shape, dt=F32):
            return ctx.enter_context(nc.sbuf_tensor(name, shape, dt))

        def sem(name):
            return ctx.enter_context(nc.semaphore(name))

        bank = [ctx.enter_context(nc.psum_tensor(f"bank{i}", [P, 512], F32)) for i in range(3)]
        quad = ctx.enter_context(nc.psum_tensor("quad", [P, 4, 512], F32))
        bank += [quad[:, i, :] for i in range(4)]
        bank.append(ctx.enter_context(nc.psum_tensor("bank7", [P, 512], F32)))

        xn_dram = nc.dram_tensor("xn_scratch", [TOK, DIM], F32).ap()
        y_dram = nc.dram_tensor("y_scratch", [SLOT_TILES * P, DIM], F32).ap()

        xs = sb("xs", [P, TT, DIM])
        xn = sb("xn", [P, TT, DIM])
        w1s = sb("w1s", [P, NE * FF])
        w2s = sb("w2s", [P, NE, FC, DIM])
        w2c = sb("w2c", [P, NE * FC * DIM])
        wrs = sb("wrs", [P, NE])
        rows = sb("rows", [96, P])
        cols = sb("cols", [P, 96])
        b2row = sb("b2row", [1, NE * DIM])
        b2p = sb("b2p", [P, NE * DIM])
        g2b = sb("g2b", [P, NE * DIM])
        be2b = sb("be2b", [P, NE * DIM])
        brb = sb("brb", [P, NE])
        b1lo = sb("b1lo", [32, P])
        b1hi = sb("b1hi", [32, 3, P], BF16)
        b1p = sb("b1p", [3, NE * FF], BF16)

        ident = sb("ident", [P, P])
        ones = sb("ones", [P, P])
        mean_w = sb("mean_w", [P, P])
        ones16 = sb("ones16", [P, P], BF16)
        before = sb("before", [P, P], BF16)
        eps_c = sb("eps_c", [P, 1])
        e_lt = sb("e_lt", [P, NE, NE])
        first_w = sb("first_w", [P, NE])
        lo_iota = sb("lo_iota", [P, P])
        tile_iota = sb("tile_iota", [P, 40])
        row_id = sb("row_id", [P, 1])

        xnT = sb("xnT", [P, 4, P])
        stats = sb("stats", [P, TT, 6])
        mv = sb("mv", [P, TT, 2])
        sdev = sb("sdev", [P, TT])
        rstd = sb("rstd", [P, TT])
        lg = sb("lg", [P, TT, NE])
        lg2 = sb("lg2", [P, TT, NE])
        eq = sb("eq", [P, TT, NE])
        oh = sb("oh", [P, TOPK, TT, NE])
        m12 = sb("m12", [P, TOPK, TT])
        mw = sb("mw", [P, TT])
        picked = sb("picked", [P, TT, NE], BF16)
        gate = sb("gate", [P, TOPK, TT])
        gden = sb("gden", [P, TT])
        ntile = sb("ntile", [P, NE])
        ntile_i = sb("ntile_i", [P, NE], I32)
        start = sb("start", [P, NE])
        end = sb("end", [P, NE])
        tri = sb("tri", [P, NE, NE])
        rank = sb("rank", [P, TT, NE])
        posf = sb("posf", [P, TOPK * TT])
        posi = sb("posi", [P, TOPK * TT], I32)
        hi_i = sb("hi_i", [P, TOPK * TT], I32)
        hi_f = sb("hi_f", [P, TOPK * TT])
        lo_f = sb("lo_f", [P, TOPK * TT])
        posu = sb("posu", [P, TOPK * TT], U32)
        oh_lo = sb("oh_lo", [P, TOPK * TT, P], BF16)
        oh_hi = sb("oh_hi", [P, TOPK * TT, 2, 40], BF16)
        tcol = sb("tcol", [P, TOPK * TT])
        slot_t = sb("slot_t", [P, 40])
        slot_u = sb("slot_u", [P, 40], U32)
        ecmp = sb("ecmp", [1, 40, NE])
        eidf = sb("eidf", [1, 40])
        eid = sb("eid", [1, 40], I32)

        xg = sb("xg", [P, 4, DIM])
        xT = sb("xT", [P, 2, P])
        hh = sb("hh", [P, 2, FF])
        hT = sb("hT", [P, 2, FF])
        st1 = sb("st1", [P, 2, 6])
        mv1 = sb("mv1", [P, 2, 2])
        sd1 = sb("sd1", [P, 2, 1])
        r1 = sb("r1", [P, 2, 1])
        yy = sb("yy", [P, 2, DIM])
        st2 = sb("st2", [P, 2, 6])
        mv2 = sb("mv2", [P, 2, 2])
        sd2 = sb("sd2", [P, 2, 1])
        r2 = sb("r2", [P, 2, 1])
        yn = sb("yn", [P, 2, DIM])
        yo = sb("yo", [P, 2, DIM])
        yg = sb("yg", [P, 4, TOPK, DIM])

        s_ld_x = sem("s_ld_x")
        s_ld_w = sem("s_ld_w")
        s_ld_w2 = sem("s_ld_w2")
        s_ld_w1 = sem("s_ld_w1")
        s_bc = sem("s_bc")
        s_ld_a = sem("s_ld_a")
        s_lam = sem("s_lam")
        s_const = sem("s_const")
        s_pool = sem("s_pool")
        s_dve = sem("s_dve")
        s_cols = sem("s_cols")
        s_colc = sem("s_colc")
        s_b1 = sem("s_b1")
        s_b1d = sem("s_b1d")
        s_w2g = sem("s_w2g")
        s_mean = sem("s_mean")
        s_w2c = sem("s_w2c")
        s_b2m = sem("s_b2m")
        s_b2c = sem("s_b2c")
        s_out = sem("s_out")

        ident16 = sb("ident16", [P, P], BF16)
        mask_q = sb("mask_q", [P, P], BF16)
        mask_k = sb("mask_k", [P, P], BF16)
        neg_half = sb("neg_half", [P, 32])
        wrow = sb("wrow", [P, 4, DIM])
        wqkvo = sb("wqkvo", [P, 4, DIM])
        lam_in = sb("lam_in", [P, 4, HD])
        lam_p = sb("lam_p", [P, 2, HD])
        lam_s = sb("lam_s", [P, 2])
        lam_e = sb("lam_e", [P, 2])
        neg_lam = sb("neg_lam", [P, 1])
        ast = sb("ast", [P, 2, 6])
        amv = sb("amv", [P, 2, 2])
        ave = sb("ave", [P, 2])
        ars = sb("ars", [P, 2])
        axn = sb("axn", [P, 2, DIM])
        axT = sb("axT", [P, 2 * P])
        qk = sb("qk", [P, 2, 2, DIM])
        part = sb("part", [P, 3, 2, 2 * DIM], BF16)
        q6 = sb("q6", [P, 2 * SUB, SLOTS, HD], BF16)
        k6 = sb("k6", [P, 2 * SUB, SLOTS, HD], BF16)
        vaug = sb("vaug", [P, 2, HEADS, VD + 1])
        kT = sb("kT", [P, HEADS, 2 * P], BF16)
        qT = sb("qT", [P, HEADS, 2 * P], BF16)
        qmT = sb("qmT", [P, HEADS, 2 * P], BF16)
        mx = sb("mx", [P, 2 * SUB])
        mpart = sb("mpart", [P, 3, 2 * SUB], BF16)
        prob = sb("prob", [P, 2, 2, 3 * P])
        rsum = sb("rsum", [P, 2, SUB])
        ow = sb("ow", [P, 2, SUB, VD])
        od = sb("od", [P, 2, HEADS, VD])
        osq = sb("osq", [P, 2, HEADS, VD])
        oms = sb("oms", [P, 2 * HEADS])
        orr = sb("orr", [P, 2 * HEADS])
        oT = sb("oT", [P, 2 * P])
        a_names = ("wT wTc lam lame laml var rs xn xTp xTc proj qkv clamp part kcopy qcopy kTp kTc qTp qTc s smax mparts "
                   "qmTp qmTc st prob o on msq rms onorm oTp oTc res step").split()
        A = {n: sem(f"at_{n}") for n in a_names} if "at" in stages else {}

        names = ("x_ready mv sd rstd xn xnst xnTp xnTc lgp lg top gexp gate picked rankp pos oh slotp slot eid "
                 "xg0 xg1 xg2 xg3 xTp xTc h relu bn mv1 sq1 hTp hTa hTb A ya mv2 sq2 yn yf yst0 yst1 "
                 "yg0 yg1 yg2 yg3 comb lstep lpool").split()
        sems = {k: {n: sem(f"{k}_{n}") for n in names} for k in stages if k != "at"}
        block = ctx.enter_context(nc.Block())

        NCONST = 16

        def moe_sync(sp, S, last):
            sp.wait_ge(S["xn"], TT)
            sp.dma_start(xn_dram.rearrange("(t p) d -> p t d", p=P), xn[:]).then_inc(S["xnst"], 16)
            def store(n, i, u):
                sp.wait_ge(S["yf"], n + 1)
                sp.dma_start(y_dram[bass.ds(n * P, P), :], yo[:, u, :]).then_inc(S[f"yst{u}"], 16)
            with sp.Fori(0, (SLOT_TILES - 1) // 2) as i:
                for u in range(2):
                    store(i * 2 + u, i, u)
            store(SLOT_TILES - 1, 0, 0)
            if last:
                out_t = out.rearrange("b (u p) d -> (b u) p d", p=P)
                for t in range(TT):
                    sp.wait_ge(S["comb"], t + 1)
                    sp.dma_start(out_t[t], xs[:, t, :]).then_inc(s_out, 16)

        def moe_gpsimd(pool, S):
            pool.wait_ge(S["xnst"], 16)
            pool.wait_ge(S["slot"], 1)

            def gather(n, i, u):
                pool.indirect_dma_start(out=xg[:, u, :], out_offset=None, in_=xn_dram,
                                        in_offset=bass.IndirectOffsetOnAxis(ap=slot_u[:, n:n + 1] if isinstance(n, int) else slot_u[:, bass.ds(n, 1)], axis=0)
                                        ).then_inc(S[f"xg{u}"], 16)

            def finish(n, i, u):
                e = pool.value_load(eid[0:1, bass.ds(n, 1)], min_val=0, max_val=NE - 1)
                pool.wait_ge(S["yn"], n + 1)
                if not (isinstance(n, int) and n < 2):
                    pool.wait_ge(S[f"yst{u}"], i * 16)
                pool.tensor_tensor(yo[:, u, :], yn[:, u, :], g2b[:, bass.ds(e * DIM, DIM)], ALU.mult).then_inc(S["lpool"], 1)
                pool.wait_ge(S["lpool"], n + 1)
                pool.tensor_tensor(yo[:, u, :], yo[:, u, :], be2b[:, bass.ds(e * DIM, DIM)], ALU.add).then_inc(S["yf"], 1)

            pool.wait_ge(S["eid"], 1)
            for n in range(4):
                gather(n, 0, n)
            for n in range(SLOT_TILES):
                if n + 4 < SLOT_TILES:
                    pool.wait_ge(S["xTp"], n + 1)
                    gather(n + 4, 0, n % 4)
                if n:
                    finish(n - 1, (n - 1) // 2, (n - 1) % 2)
            finish(SLOT_TILES - 1, (SLOT_TILES - 1) // 2, 0)
            pool.wait_ge(S["yst0"], 16 * ((SLOT_TILES + 1) // 2))
            pool.wait_ge(S["yst1"], 16 * (SLOT_TILES // 2))
            for t in range(TT):
                if t >= 4:
                    pool.wait_ge(S["comb"], t - 3)
                for k in range(TOPK):
                    c = k * TT + t
                    pool.indirect_dma_start(out=yg[:, t % 4, k, :], out_offset=None, in_=y_dram,
                                            in_offset=bass.IndirectOffsetOnAxis(ap=posu[:, c:c + 1], axis=0)
                                            ).then_inc(S[f"yg{t % 4}"], 16)

        def moe_scalar(act, S):
            act.wait_ge(S["mv"], TT)
            act.activation(sdev[:], mv[:, :, 1], ACT.Sqrt, bias=eps_c[:]).then_inc(S["sd"], 1)
            for g in range(4):
                act.wait_ge(S["xnTp"], g + 1)
                if g:
                    act.wait_ge(S["lgp"], g)
                act.copy(xnT[:], bank[g % 2][:].rearrange("p (a b) -> p a b", a=4)).then_inc(S["xnTc"], 1)
            act.wait_ge(S["top"], 1)
            act.activation(gden[:], mw[:], ACT.Exp).then_inc(S["gexp"], 1)

            def copy_xT(m, u):
                act.wait_ge(S["xTp"], m + 1)
                if not (isinstance(m, int) and m < 2):
                    act.wait_ge(S["h"], m - 1)
                act.copy(xT[:, u, :], bank[0][:, 0:P]).then_inc(S["xTc"], 1)

            def relu(m, u):
                act.wait_ge(S["h"], m + 1)
                if not (isinstance(m, int) and m < 2):
                    act.wait_ge(S["hTp"], m - 1)
                    act.wait_ge(S["bn"], m - 1)
                act.activation(hh[:, u, :], bank[1 + u][:], ACT.Relu).then_inc(S["relu"], 1)

            def sqrt1(m, u):
                act.wait_ge(S["mv1"], m + 1)
                act.activation(sd1[:, u, :], mv1[:, u, 1:2], ACT.Sqrt, bias=eps_c[:]).then_inc(S["sq1"], 1)

            def sqrt2(m, u):
                act.wait_ge(S["mv2"], m + 1)
                act.activation(sd2[:, u, :], mv2[:, u, 1:2], ACT.Sqrt, bias=eps_c[:]).then_inc(S["sq2"], 1)

            def body(n, u, do_x=True, do_h=True, lag=True):
                act.wait_ge(S["hTp"], n + 1)
                if not (isinstance(n, int) and n < 2):
                    act.wait_ge(S["A"], n - 1)
                act.copy(hT[:, u, 0:256], bank[3][:, 0:256]).then_inc(S["hTa"], 1)
                if do_x:
                    copy_xT(n + 2, u)
                if lag:
                    sqrt2(n - 1, 1 - u)
                if do_h:
                    relu(n + 1, 1 - u)
                    sqrt1(n + 1, 1 - u)

            copy_xT(0, 0)
            copy_xT(1, 1)
            relu(0, 0)
            sqrt1(0, 0)
            body(0, 0, lag=False)
            body(1, 1)
            with act.Fori(1, (SLOT_TILES - 3) // 2) as i:
                for u in range(2):
                    body(i * 2 + u, u)
            for n in range(SLOT_TILES - 3, SLOT_TILES):
                body(n, n % 2, do_x=n + 2 < SLOT_TILES, do_h=n + 1 < SLOT_TILES)
            sqrt2(SLOT_TILES - 1, (SLOT_TILES - 1) % 2)

        def moe_tensor(pe, S, first):
            pe.wait_ge(s_const, NCONST)
            for g in range(4):
                pe.wait_ge(S["xn"], 4 * g + 4)
                if g >= 2:
                    pe.wait_ge(S["xnTc"], g - 1)
                for j in range(4):
                    last = pe.transpose(bank[g % 2][:, j * P:(j + 1) * P], xn[:, 4 * g + j, :], ident[:])
                last.then_inc(S["xnTp"], 1)
                pe.wait_ge(S["xnTc"], g + 1)
                for j in range(4):
                    t = 4 * g + j
                    last = pe.matmul(bank[2][:, t * NE:(t + 1) * NE], xnT[:, j, :], wrs[:], start=True, stop=True)
                last.then_inc(S["lgp"], 1)
            pe.wait_ge(S["picked"], 1)
            pe.matmul(bank[3][:, 0:NE], before[:], picked[:, 0, :], start=True, stop=True)
            pe.matmul(bank[3][:, NE:TT * NE], before[:], picked[:, 1:TT, :], start=True, stop=False)
            for t in range(TT - 2, -1, -1):
                w = TT - 1 - t
                pe.matmul(bank[3][:, (t + 1) * NE:TT * NE].rearrange("p (a b) -> p a b", b=NE), ones16[:],
                          picked[:, t:t + 1, :].to_broadcast([P, w, NE]), start=False, stop=(t == 0),
                          skip_group_check=(t > 0))
            for t in range(TT):
                last = pe.matmul(bank[4][:, 0:NE], ones16[:], picked[:, t, :], start=(t == 0), stop=(t == TT - 1))
            last.then_inc(S["rankp"], 1)
            for c in range(TOPK * TT):
                if c % 8 == 0:
                    pe.wait_ge(S["oh"], c // 8 + 1)
                last = pe.matmul(bank[5][:, 0:80], oh_lo[:, c, :], oh_hi[:, c, :, :], start=(c == 0), stop=(c == TOPK * TT - 1))
            last.then_inc(S["slotp"], 1)
            pe.wait_ge(S["eid"], 1)
            if first:
                weights_tensor(pe)
                pe.wait_ge(s_ld_w1, 16)
            pe.wait_ge(s_w2c, 2)
            pe.wait_ge(s_b1d, 48)
            pe.wait_ge(s_b2c, 1)

            def turn_x(m, i, q):
                pe.wait_ge(S[f"xg{q}"], i * 16 + 16)
                if not (isinstance(m, int) and m == 0):
                    pe.wait_ge(S["xTc"], m)
                pe.transpose(bank[0][:, 0:P], xg[:, q, :], ident[:]).then_inc(S["xTp"], 1)

            def hidden(m, u):
                e = pe.value_load(eid[0:1, bass.ds(m, 1)], min_val=0, max_val=NE - 1)
                pe.wait_ge(S["xTc"], m + 1)
                if not (isinstance(m, int) and m < 2):
                    pe.wait_ge(S["relu"], m - 1)
                pe.matmul(bank[1 + u][:], ones16[0:3, :], b1p[:, bass.ds(e * FF, FF)], start=True, stop=False)
                pe.matmul(bank[1 + u][:], xT[:, u, :], w1s[:, bass.ds(e * FF, FF)], start=False, stop=True).then_inc(S["h"], 1)

            def turn_h(n, u):
                pe.wait_ge(S["relu"], n + 1)
                if not (isinstance(n, int) and n == 0):
                    pe.wait_ge(S["hTa"], n)
                    pe.wait_ge(S["hTb"], n)
                for c in range(FC):
                    last = pe.transpose(bank[3 + c // 2][:, c % 2 * P:c % 2 * P + P], hh[:, u, c * P:(c + 1) * P], ident[:])
                last.then_inc(S["hTp"], 1)

            def second(n, u):
                e = pe.value_load(eid[0:1, bass.ds(n, 1)], min_val=0, max_val=NE - 1)
                pe.wait_ge(S["hTa"], n + 1)
                pe.wait_ge(S["hTb"], n + 1)
                if not (isinstance(n, int) and n < 2):
                    pe.wait_ge(S["ya"], n - 1)
                for c in range(FC):
                    last = pe.matmul(bank[5 + u][:, 0:DIM], hT[:, u, c * P:(c + 1) * P],
                                     w2c[:, bass.ds(e * (FC * DIM) + c * DIM, DIM)], start=(c == 0), stop=(c == FC - 1))
                last.then_inc(S["A"], 1)

            def body(n, i, q, do_x=True, do_h=True):
                turn_h(n, q % 2)
                if do_x:
                    turn_x(n + 2, i + (q + 2) // 4, (q + 2) % 4)
                if do_h:
                    hidden(n + 1, 1 - q % 2)
                second(n, q % 2)

            turn_x(0, 0, 0)
            turn_x(1, 0, 1)
            hidden(0, 0)
            for n in range(4):
                body(n, 0, n)
            with pe.Fori(1, (SLOT_TILES - 3) // 4) as i:
                for q in range(4):
                    body(i * 4 + q, i, q)
            for n in range(SLOT_TILES - 3, SLOT_TILES):
                body(n, n // 4, n % 4, do_x=n + 2 < SLOT_TILES, do_h=n + 1 < SLOT_TILES)

        def moe_vector(dve, S, step, first):
            if first:
                dve.wait_ge(s_ld_x, 16)
            for t in range(TT):
                dve.bn_stats(stats[:, t, :], xs[:, t, :]).then_inc(S["lstep"], 1)
            for t in range(TT):
                dve.wait_ge(S["lstep"], t + 1)
                dve.bn_aggr(mv[:, t, :], stats[:, t, :]).then_inc(S["mv"], 1)
            dve.wait_ge(S["sd"], 1)
            step(dve.reciprocal(rstd[:], sdev[:]))
            for t in range(TT):
                dve.tensor_scalar(xn[:, t, :], xs[:, t, :], mv[:, t, 0:1], rstd[:, t:t + 1],
                                  ALU.subtract, ALU.mult).then_inc(S["xn"], 1)
            dve.wait_ge(S["lgp"], 4)
            dve.wait_ge(s_const, NCONST)
            step(dve.tensor_tensor(lg[:], bank[2][:, 0:TT * NE].rearrange("p (a b) -> p a b", b=NE),
                                   brb[:, None, :].to_broadcast([P, TT, NE]), ALU.add))
            for k in range(TOPK):
                src = lg if k == 0 else lg2
                step(dve.tensor_reduce(m12[:, k, :], src[:], X, ALU.max))
                step(dve.tensor_tensor(eq[:], src[:], m12[:, k, :, None].to_broadcast([P, TT, NE]), ALU.is_equal))
                step(dve.tensor_tensor(eq[:], eq[:], first_w[:, None, :].to_broadcast([P, TT, NE]), ALU.mult))
                step(dve.tensor_reduce(mw[:], eq[:], X, ALU.max))
                step(dve.tensor_tensor(oh[:, k], eq[:], mw[:, :, None].to_broadcast([P, TT, NE]), ALU.is_equal))
                if k == 0:
                    step(dve.scalar_tensor_tensor(lg2[:], oh[:, 0], -BIG, lg[:], ALU.mult, ALU.add))
            dve.tensor_tensor(picked[:], oh[:, 0], oh[:, 1], ALU.add).then_inc(S["picked"], 1)
            dve.tensor_tensor(mw[:], m12[:, 1, :], m12[:, 0, :], ALU.subtract).then_inc(S["top"], 1)
            dve.wait_ge(S["rankp"], 1)
            step(dve.tensor_scalar(ntile_i[:], bank[4][:, 0:NE], float(P - 1), None, ALU.add))
            step(dve.tensor_scalar(ntile_i[:], ntile_i[:], 7, None, ALU.arith_shift_right))
            step(dve.tensor_copy(ntile[:], ntile_i[:]))
            step(dve.tensor_tensor(tri[:], e_lt[:], ntile[:, None, :].to_broadcast([P, NE, NE]), ALU.mult))
            step(dve.tensor_reduce(start[:], tri[:], X, ALU.add))
            step(dve.tensor_tensor(end[:], start[:], ntile[:], ALU.add))
            step(dve.scalar_tensor_tensor(rank[:], start[:, None, :].to_broadcast([P, TT, NE]), float(P),
                                          bank[3][:, 0:TT * NE].rearrange("p (a b) -> p a b", b=NE), ALU.mult, ALU.add))
            for k in range(TOPK):
                step(dve.tensor_tensor(eq[:], oh[:, k], rank[:], ALU.mult))
                step(dve.tensor_reduce(posf[:, k * TT:(k + 1) * TT], eq[:], X, ALU.add))
            step(dve.tensor_copy(posi[:], posf[:]))
            dve.tensor_copy(posu[:], posf[:]).then_inc(S["pos"], 1)
            step(dve.tensor_scalar(hi_i[:], posi[:], 7, None, ALU.arith_shift_right))
            step(dve.tensor_copy(hi_f[:], hi_i[:]))
            step(dve.scalar_tensor_tensor(lo_f[:], hi_f[:], -float(P), posf[:], ALU.mult, ALU.add))
            for q in range(4):
                c = slice(8 * q, 8 * q + 8)
                step(dve.tensor_tensor(oh_lo[:, c, :], lo_f[:, c, None].to_broadcast([P, 8, P]),
                                       lo_iota[:, None, :].to_broadcast([P, 8, P]), ALU.is_equal))
                step(dve.tensor_tensor(oh_hi[:, c, 1, :], hi_f[:, c, None].to_broadcast([P, 8, 40]),
                                       tile_iota[:, None, :].to_broadcast([P, 8, 40]), ALU.is_equal))
                step(dve.tensor_tensor(oh_hi[:, c, 0, :], oh_hi[:, c, 1, :],
                                       tcol[:, c, None].to_broadcast([P, 8, 40]), ALU.mult))
                dve.tensor_scalar(oh_hi[:, c, 1, :], oh_hi[:, c, 1, :], row_id[:], None, ALU.mult).then_inc(S["oh"], 1)
            step(dve.tensor_tensor(ecmp[:], tile_iota[0:1, :, None].to_broadcast([1, 40, NE]),
                                   end[0:1, None, :].to_broadcast([1, 40, NE]), ALU.is_ge))
            step(dve.tensor_reduce(eidf[:], ecmp[:], X, ALU.add))
            dve.tensor_scalar(eid[:], eidf[:], float(NE - 1), None, ALU.min).then_inc(S["eid"], 1)
            dve.wait_ge(S["slotp"], 1)
            step(dve.tensor_copy(slot_t[:], bank[5][:, 40:80]))
            dve.scalar_tensor_tensor(slot_u[:], bank[5][:, 0:40], float(P), slot_t[:], ALU.mult, ALU.add).then_inc(S["slot"], 1)
            dve.wait_ge(S["gexp"], 1)
            step(dve.tensor_scalar(m12[:, 0, :], gden[:], 2.0, 2.0, ALU.mult, ALU.add))
            step(dve.reciprocal(gate[:, 0, :], m12[:, 0, :]))
            dve.tensor_tensor(gate[:, 1, :], gate[:, 0, :], gden[:], ALU.mult).then_inc(S["gate"], 1)
            if first:
                weights_vector(dve, step)

            ls = LoopSteps(dve, S["lstep"])
            PER = 4

            def stats1(m, u):
                dve.wait_ge(S["relu"], m + 1)
                if not (isinstance(m, int) and m < 2):
                    dve.wait_ge(S["sq1"], m - 1)
                dve.bn_stats(st1[:, u, :], hh[:, u, :]).then_inc(S["bn"], 1)
                dve.wait_ge(S["bn"], m + 1)
                dve.memset(hold[:, 0:1], 0.0)
                dve.bn_aggr(mv1[:, u, :], st1[:, u, :]).then_inc(S["mv1"], 1)

            def evac(n, u):
                dve.wait_ge(S["hTp"], n + 1)
                if not (isinstance(n, int) and n < 2):
                    dve.wait_ge(S["A"], n - 1)
                dve.tensor_copy(hT[:, u, 256:512], bank[4][:, 0:256]).then_inc(S["hTb"], 1)

            def y_part(m, u):
                e = dve.value_load(eid[0:1, bass.ds(m, 1)], min_val=0, max_val=NE - 1)
                ls.start(m * PER + TT)
                dve.wait_ge(S["sq1"], m + 1)
                ls(dve.reciprocal(r1[:, u, :], sd1[:, u, :]))
                dve.wait_ge(S["A"], m + 1)
                dve.scalar_tensor_tensor(yy[:, u, :], bank[5 + u][:, 0:DIM], r1[:, u, :],
                                         b2p[:, bass.ds(e * DIM, DIM)], ALU.mult, ALU.add).then_inc(S["ya"], 1)
                dve.wait_ge(S["ya"], m + 1)
                ls(dve.tensor_scalar(yy[:, u, :], yy[:, u, :], 0.0, None, ALU.max))
                dve.bn_stats(st2[:, u, :], yy[:, u, :]).then_inc(S["lstep"], 1)
                dve.wait_ge(S["lstep"], m * PER + TT + 3)
                dve.memset(hold[:, 1:2], 0.0)
                dve.bn_aggr(mv2[:, u, :], st2[:, u, :]).then_inc(S["mv2"], 1)

            def y_norm(m, u):
                ls.base, ls.n = m * PER + TT, 3
                dve.wait_ge(S["sq2"], m + 1)
                ls(dve.reciprocal(r2[:, u, :], sd2[:, u, :]))
                if not (isinstance(m, int) and m < 2):
                    dve.wait_ge(S["yf"], m - 1)
                dve.tensor_scalar(yn[:, u, :], yy[:, u, :], mv2[:, u, 0:1], r2[:, u, :],
                                  ALU.subtract, ALU.mult).then_inc(S["yn"], 1)

            def body(n, u, do_h=True, lag=True):
                evac(n, u)
                if lag:
                    y_part(n - 1, 1 - u)
                if do_h:
                    stats1(n + 1, 1 - u)
                if lag:
                    y_norm(n - 1, 1 - u)

            stats1(0, 0)
            body(0, 0, lag=False)
            body(1, 1)
            body(2, 0)
            body(3, 1)
            with dve.Fori(2, (SLOT_TILES - 1) // 2) as i:
                for u in range(2):
                    body(i * 2 + u, u)
            body(SLOT_TILES - 1, 0, do_h=False)
            y_part(SLOT_TILES - 1, 0)
            y_norm(SLOT_TILES - 1, 0)

            base = TT + PER * SLOT_TILES
            for t in range(TT):
                dve.wait_ge(S[f"yg{t % 4}"], 32 * (t // 4 + 1))
                dve.scalar_tensor_tensor(xs[:, t, :], yg[:, t % 4, 0, :], gate[:, 0, t:t + 1], xs[:, t, :],
                                         ALU.mult, ALU.add).then_inc(S["lstep"], 1)
                dve.wait_ge(S["lstep"], base + t + 1)
                dve.scalar_tensor_tensor(xs[:, t, :], yg[:, t % 4, 1, :], gate[:, 1, t:t + 1], xs[:, t, :],
                                         ALU.mult, ALU.add).then_inc(S["comb"], 1)

        def att_gpsimd(pool):
            with pool.Fori(0, BATCH) as b:
                pool.wait_ge(A["var"], b + 1)
                pool.tensor_tensor(ars[:], ave[:], neg_half[:, 0:2], ALU.pow).then_inc(A["rs"], 1)
                pool.wait_ge(A["part"], b + 1)
                pool.tensor_tensor(gpad[:, 1:2], neg_half[0:1, 0:1], neg_half[0:1, 0:1], ALU.mult)
                for j, at in ((0, slice(0, 4, 3)), (0, slice(5, 6)), (1, slice(1, 5, 3)), (2, slice(2, 3))):
                    n = len(range(*at.indices(8)))
                    last = pool.tensor_copy(k6[:, :, at, :], part[:, j, 1, :].rearrange("p (a e) -> p a e", e=HD)[:, :, None, :]
                                            .to_broadcast([P, 2 * SUB, n, HD]))
                last.then_inc(A["kcopy"], 1)
                pool.wait_ge(A["msq"], b + 1)
                pool.tensor_tensor(orr[:], oms[:], neg_half[:, 0:2 * HEADS], ALU.pow).then_inc(A["rms"], 1)

        def att_scalar(act):
            act.wait_ge(A["wT"], 1)
            act.copy(wqkvo[:].rearrange("p a b -> p (a b)"), bank[7][:]).then_inc(A["wTc"], 1)
            act.wait_ge(A["lam"], 1)
            act.activation(lam_e[:], lam_s[:], ACT.Exp).then_inc(A["lame"], 1)
            with act.Fori(0, BATCH) as b:
                act.wait_ge(A["xTp"], b + 1)
                act.copy(axT[:], bank[0][:, 0:2 * P]).then_inc(A["xTc"], 1)
                for u in range(2):
                    act.wait_ge(A["proj"], b * 2 + u + 1)
                    act.activation(qk[:, 0, u, :], bank[1][:, 0:DIM], ACT.Copy, scale=HD ** -0.5)
                    act.copy(qk[:, 1, u, :], bank[1][:, DIM:2 * DIM])
                    act.copy(vaug[:, u, :, 0:VD], bank[1][:, 2 * DIM:3 * DIM].rearrange("p (a e) -> p a e", e=VD)).then_inc(A["qkv"], 1)
                for u in range(2):
                    act.wait_ge(A["kTp"], b * 2 + u + 1)
                    act.copy(kT[:, :, u * P:u * P + P], bank[2][:].bitcast(BF16).rearrange("p (a e) -> p a e", e=P)).then_inc(A["kTc"], 1)
                for u in range(2):
                    act.wait_ge(A["qmTp"], b * 2 + u + 1)
                    act.copy(qmT[:, :, u * P:u * P + P], bank[2][:].bitcast(BF16).rearrange("p (a e) -> p a e", e=P)).then_inc(A["qmTc"], 1)
                for g in range(HEADS):
                    act.wait_ge(A["st"], b * 8 + g + 1)
                    if g >= 2:
                        act.wait_ge(A["o"], b * 8 + g - 1)
                    act.activation(prob[:, g % 2], quad[:, g % 2 * 2:g % 2 * 2 + 2, 0:3 * P], ACT.Exp).then_inc(A["prob"], 1)
                act.wait_ge(A["oTp"], b + 1)
                act.copy(oT[:], bank[1][:, 0:2 * P]).then_inc(A["oTc"], 1)

        def att_tensor(pe):
            pe.wait_ge(s_ld_a, 80)
            for j in range(4):
                last = pe.transpose(bank[7][:, j * P:(j + 1) * P], wrow[:, j, :], ident[:])
            last.then_inc(A["wT"], 1)

            def turn8(src, u):
                for hp in range(HEADS):
                    last = pe.transpose(bank[2 + 0 if src is not q6 else 2][:].bitcast(BF16)[:, hp * P:hp * P + P],
                                        src[:, u * SUB + 2 * hp:u * SUB + 2 * hp + 2].rearrange("p a s e -> p (a s e)"), ident16[:])
                return last

            with pe.Fori(0, BATCH) as b:
                pe.wait_ge(A["xn"], b + 1)
                for u in range(2):
                    last = pe.transpose(bank[0][:, u * P:u * P + P], axn[:, u, :], ident[:])
                last.then_inc(A["xTp"], 1)
                pe.wait_ge(A["xTc"], b + 1)
                for u in range(2):
                    if u:
                        pe.wait_ge(A["qkv"], b * 2 + 1)
                    pe.matmul(bank[1][:, 0:3 * DIM], axT[:, u * P:u * P + P], wqkvo[:, 0:3, :], start=True, stop=True).then_inc(A["proj"], 1)
                pe.wait_ge(A["kcopy"], b + 1)
                for u in range(2):
                    if u:
                        pe.wait_ge(A["kTc"], b * 2 + 1)
                    turn8(k6, u).then_inc(A["kTp"], 1)
                pe.wait_ge(A["kTc"], b * 2 + 2)
                pe.wait_ge(A["qcopy"], b + 1)
                for u in range(2):
                    if u:
                        pe.wait_ge(A["qTc"], b * 2 + 1)
                    turn8(q6, u).then_inc(A["qTp"], 1)
                pe.wait_ge(A["qTc"], b * 2 + 2)
                for n in range(6):
                    u, h0, per = (0, 8 * n, 4) if n < 2 else (1, 4 * (n - 2), 2)
                    w = (u + 1) * P
                    if n >= 2:
                        pe.wait_ge(A["smax"], b * 6 + n - 1)
                    for a in range(per):
                        hs = [(h, slice(64 * (h % 2), 64 * (h % 2) + MAXSLOT * HD), quad[:, n % 2 * 2 + h % 2, a * w:(a + 1) * w])
                              for h in (h0 + 2 * a, h0 + 2 * a + 1)]
                        if u:
                            for h, r, o in hs:
                                pe.matmul(o[:, 0:P], qT[r, h // 2, P:2 * P], kT[r, h // 2, 0:P], start=True, stop=True)
                        for h, r, o in hs:
                            pe.matmul(o[:, w - P:w], ident16[:], mask_q[:], start=True, stop=False)
                        for h, r, o in hs:
                            last = pe.matmul(o[:, w - P:w], qT[r, h // 2, u * P:u * P + P], kT[r, h // 2, u * P:u * P + P],
                                             start=False, stop=True)
                    last.then_inc(A["s"], 1)
                pe.wait_ge(A["mparts"], b + 1)
                for u in range(2):
                    if u:
                        pe.wait_ge(A["qmTc"], b * 2 + 1)
                    turn8(q6, u).then_inc(A["qmTp"], 1)
                pe.wait_ge(A["qmTc"], b * 2 + 2)

                def scores_t(g):
                    if g >= 2:
                        pe.wait_ge(A["prob"], b * 8 + g - 1)
                    hs = [(slice(64 * p, 64 * p + 64), quad[:, g % 2 * 2 + p, :]) for p in range(2)]
                    for r, o in hs:
                        pe.matmul(o[:, P:2 * P], kT[r, g, 0:P], qmT[r, g, P:2 * P], start=True, stop=True)
                    for r, o in hs:
                        pe.matmul(o.rearrange("p (a e) -> p a e", e=2 * P)[:, :, 0:P], ident16[:],
                                  mask_k[:, None, :].to_broadcast([P, 2, P]), start=True, stop=False)
                    for r, o in hs:
                        pe.matmul(o[:, 0:P], kT[r, g, 0:P], qmT[r, g, 0:P], start=False, stop=False)
                    for r, o in hs:
                        last = pe.matmul(o[:, 2 * P:3 * P], kT[r, g, P:2 * P], qmT[r, g, P:2 * P], start=False, stop=True)
                    last.then_inc(A["st"], 1)

                def values(g):
                    pe.wait_ge(A["prob"], b * 8 + g + 1)
                    v0, v1 = (vaug[:, u, g, :] for u in range(2))
                    for p in range(2):
                        c = slice((2 * g + p) * (VD + 1), (2 * g + p + 1) * (VD + 1))
                        pr = prob[:, g % 2, p, :]
                        pe.matmul(bank[7][:, c], pr[:, 0:P], v0, start=True, stop=True)
                        pe.matmul(bank[0][:, c], pr[:, P:2 * P], v0, start=True, stop=False)
                        last = pe.matmul(bank[0][:, c], pr[:, 2 * P:3 * P], v1, start=False, stop=True)
                    last.then_inc(A["o"], 1)

                for g in range(HEADS + 1):
                    if g < HEADS:
                        scores_t(g)
                    if g:
                        values(g - 1)
                pe.wait_ge(A["onorm"], b + 1)
                for u in range(2):
                    last = pe.transpose(bank[1][:, u * P:u * P + P], od[:, u].rearrange("p a e -> p (a e)"), ident[:])
                last.then_inc(A["oTp"], 1)
                pe.wait_ge(A["oTc"], b + 1)
                for u in range(2):
                    last = pe.matmul(bank[1][:, (2 + u) * P:(3 + u) * P], oT[:, u * P:u * P + P], wqkvo[:, 3, :], start=True, stop=True)
                last.then_inc(A["res"], 1)

        def att_vector(dve, step):
            dve.wait_ge(s_ld_a, 80)
            step(dve.tensor_tensor(lam_p[:], lam_in[:, 0:4:2, :], lam_in[:, 1:4:2, :], ALU.mult))
            dve.tensor_reduce(lam_s[:], lam_p[:], X, ALU.add).then_inc(A["lam"], 1)
            dve.wait_ge(A["lame"], 1)
            step(dve.tensor_tensor(neg_lam[:], lam_e[:, 1:2], lam_e[:, 0:1], ALU.subtract))
            step(dve.tensor_scalar(neg_lam[:], neg_lam[:], -LAMBDA_INIT, None, ALU.add))
            dve.wait_ge(A["wTc"], 1)
            ls = LoopSteps(dve, A["step"])
            with dve.Fori(0, BATCH) as b:
                ls.start(b * ATT_STEPS)
                for u in range(2):
                    ls(dve.bn_stats(ast[:, u, :], xs[:, bass.ds(b * 2 + u, 1), :]))
                    dve.memset(hold[:, u:u + 1], 0.0)
                    dve.bn_aggr(amv[:, u, :], ast[:, u, :]).then_inc(A["step"], 1)
                    ls.n += 1
                dve.wait_ge(A["step"], ls.base + ls.n)
                dve.tensor_scalar(ave[:], amv[:, :, 1], EPS, None, ALU.add).then_inc(A["var"], 1)
                dve.wait_ge(A["rs"], b + 1)
                for u in range(2):
                    last = dve.tensor_scalar(axn[:, u, :], xs[:, bass.ds(b * 2 + u, 1), :].rearrange("p a e -> p (a e)"),
                                             amv[:, u, 0:1], ars[:, u:u + 1], ALU.subtract, ALU.mult)
                last.then_inc(A["xn"], 1)
                dve.wait_ge(A["qkv"], b * 2 + 2)
                qk2 = qk[:].rearrange("p a u e -> p a (u e)")
                ls(dve.tensor_scalar(qk2, qk2, GUARD, -GUARD, ALU.min, ALU.max))
                ls(dve.tensor_copy(part[:, 0], qk2))
                ls(dve.tensor_tensor(qk2, qk2, part[:, 0], ALU.subtract))
                ls(dve.tensor_copy(part[:, 1], qk2))
                ls(dve.tensor_tensor(qk2, qk2, part[:, 1], ALU.subtract))
                dve.tensor_copy(part[:, 2], qk2).then_inc(A["part"], 1)
                dve.wait_ge(A["part"], b + 1)
                for j, lo, n in ((0, 0, 3), (1, 3, 2), (2, 5, 1)):
                    last = dve.tensor_copy(q6[:, :, lo:lo + n, :], part[:, j, 0, :].rearrange("p (a e) -> p a e", e=HD)[:, :, None, :]
                                           .to_broadcast([P, 2 * SUB, n, HD]))
                last.then_inc(A["qcopy"], 1)
                for u in range(2):
                    dve.wait_ge(A["qTp"], b * 2 + u + 1)
                    dve.tensor_copy(qT[:, :, u * P:u * P + P], bank[2][:].bitcast(BF16).rearrange("p (a e) -> p a e", e=P)).then_inc(A["qTc"], 1)
                for n in range(6):
                    u, h0, per = (0, 8 * n, 4) if n < 2 else (1, 4 * (n - 2), 2)
                    dve.wait_ge(A["s"], b * 6 + n + 1)
                    c = u * SUB + h0
                    dve.tensor_reduce(mx[:, c:c + 2 * per].rearrange("p (a q) -> p q a", q=2),
                                      quad[:, n % 2 * 2:n % 2 * 2 + 2, :].rearrange("p q (a e) -> p q a e", a=per), X, ALU.max
                                      ).then_inc(A["smax"], 1)
                dve.wait_ge(A["smax"], b * 6 + 6)
                ls(dve.tensor_scalar(mx[:], mx[:], -1.0, None, ALU.mult))
                for j in range(3):
                    ls(dve.tensor_copy(mpart[:, j, :], mx[:]))
                    if j < 2:
                        ls(dve.tensor_tensor(mx[:], mx[:], mpart[:, j, :], ALU.subtract))
                dve.tensor_copy(q6[:, :, MAXSLOT, 0:3], mpart[:].rearrange("p j a -> p a j")).then_inc(A["mparts"], 1)
                dve.wait_ge(A["o"], b * 8 + 8)
                for u in range(2):
                    ob = bank[7 if u == 0 else 0][:, 0:SUB * (VD + 1)].rearrange("p (a e) -> p a e", e=VD + 1)
                    ls(dve.reciprocal(rsum[:, u, :], ob[:, :, VD]))
                    ls(dve.tensor_scalar(rsum[:, u, 1:SUB:2], rsum[:, u, 1:SUB:2], neg_lam[:], None, ALU.mult))
                    ls(dve.tensor_tensor(ow[:, u], ob[:, :, 0:VD], rsum[:, u, :, None].to_broadcast([P, SUB, VD]), ALU.mult))
                owv = ow[:].rearrange("p u a e -> p (u a) e")
                odv = od[:].rearrange("p u a e -> p (u a) e")
                ls(dve.tensor_tensor(odv, owv[:, 0:2 * SUB:2, :], owv[:, 1:2 * SUB:2, :], ALU.add))
                osv = osq[:].rearrange("p u a e -> p (u a) e")
                ls(dve.tensor_tensor(osv, odv, odv, ALU.mult))
                ls(dve.tensor_reduce(oms[:], osv, X, ALU.add))
                dve.tensor_scalar(oms[:], oms[:], 1.0 / VD, EPS, ALU.mult, ALU.add).then_inc(A["msq"], 1)
                dve.wait_ge(A["rms"], b + 1)
                ls(dve.tensor_scalar(orr[:], orr[:], 1.0 - LAMBDA_INIT, None, ALU.mult))
                dve.tensor_tensor(odv, odv, orr[:, :, None].to_broadcast([P, 2 * HEADS, VD]), ALU.mult).then_inc(A["onorm"], 1)
                dve.wait_ge(A["res"], b + 1)
                ls(dve.tensor_tensor(xs[:, bass.ds(b * 2, 2), :], xs[:, bass.ds(b * 2, 2), :],
                                     bank[1][:, 2 * P:4 * P].rearrange("p (a e) -> p a e", e=DIM), ALU.add))
                assert ls.n == ATT_STEPS, ls.n

        def weights_vector(dve, step):
            dve.wait_ge(s_ld_w, 16 * 6)
            step(dve.tensor_copy(b1hi[:, 0, :], b1s[:]))
            step(dve.tensor_tensor(b1lo[:], b1s[:], b1hi[:, 0, :], ALU.subtract))
            step(dve.tensor_copy(b1hi[:, 1, :], b1lo[:]))
            step(dve.tensor_tensor(b1lo[:], b1lo[:], b1hi[:, 1, :], ALU.subtract))
            dve.tensor_copy(b1hi[:, 2, :], b1lo[:]).then_inc(s_b1, 1)
            w2cv = w2c[:].rearrange("p (a c d) -> p a c d", a=NE, c=FC)
            dve.wait_ge(s_b2m, 1)
            for h in range(2):
                step(dve.tensor_copy(b2p[:, 512 * h:512 * h + 512], bank[6 + h][:]))
            dve.engine_nop().then_inc(s_b2c, 1) if False else dve.sem_inc(s_b2c, 1)
            dve.wait_ge(s_w2g, 2)
            for h in range(2):
                dve.wait_ge(s_mean, h + 1)
                for a in range(4):
                    e = 4 * h + a
                    ins = dve.tensor_tensor(w2cv[:, e], w2cv[:, e],
                                            bank[1 + h][:, None, a * DIM:(a + 1) * DIM].to_broadcast([P, FC, DIM]), ALU.subtract)
                    if a < 3:
                        step(ins)
                ins.then_inc(s_w2c, 1)

        def weights_tensor(pe):
            pe.wait_ge(s_colc, 1)
            pe.wait_ge(s_ld_w2, 16)
            for h in range(2):
                for a in range(4):
                    e = 4 * h + a
                    o = bank[6 + h][:, a * DIM:(a + 1) * DIM]
                    for c in range(FC):
                        j = 32 + e * FC + c
                        pe.matmul(o, cols[:, j:j + 1].to_broadcast([P, P]), w2s[:, e, c, :], start=(c == 0), stop=False)
                    last = pe.matmul(o, ones[0:1, :], b2row[:, e * DIM:(e + 1) * DIM], start=False, stop=True)
            last.then_inc(s_b2m, 1)
            w2cv = w2c[:].rearrange("p (a c d) -> p a c d", a=NE, c=FC)
            for h in range(2):
                pe.wait_ge(s_w2g, h + 1)
                for c in range(FC):
                    last = pe.matmul(bank[1 + h][:].rearrange("p (a d) -> p a d", d=DIM), mean_w[:],
                                     w2cv[:, 4 * h:4 * h + 4, c, :], start=(c == 0), stop=(c == FC - 1))
                last.then_inc(s_mean, 1)

        b1s = sb("b1s", [32, P])
        hold = sb("hold", [1, 2])
        gpad = sb("gpad", [1, 2])

        @block.sync
        def _(sp):
            sp.dma_start(xs[:], x.rearrange("b (u p) d -> p (b u) d", p=P)).then_inc(s_ld_x, 16)
            sp.dma_start(wrs[:], Wr).then_inc(s_ld_w, 16)
            sp.dma_start(rows[0:32, :], g1.rearrange("a (c p) -> (a c) p", p=P)).then_inc(s_ld_w, 16)
            sp.dma_start(rows[32:64, :], be1.rearrange("a (c p) -> (a c) p", p=P)).then_inc(s_ld_w, 16)
            sp.dma_start(rows[64:96, :], b1.rearrange("a (c p) -> (a c) p", p=P)).then_inc(s_ld_w, 16)
            sp.dma_start(b1s[:], b1.rearrange("a (c p) -> (a c) p", p=P)).then_inc(s_ld_w, 16)
            sp.dma_start(b2row[:], b2.rearrange("(o a) d -> o (a d)", o=1)).then_inc(s_ld_w, 16)
            sp.dma_start(w2s[:].rearrange("p a c d -> p (a c) d"), W2.rearrange("a (c p) d -> p (a c) d", p=P)).then_inc(s_ld_w2, 16)
            sp.dma_start(w1s[:].rearrange("p (a f) -> p a f", a=NE), W1.rearrange("a p f -> p a f")).then_inc(s_ld_w1, 16)
            for j, w in enumerate((Wq, Wk, Wv, Wo)):
                sp.dma_start(wrow[:, j, :], w).then_inc(s_ld_a, 16)
            sp.wait_ge(s_b1, 1)
            for j in range(3):
                sp.dma_start(b1p[j:j + 1, :], b1hi[:, j, :]).then_inc(s_b1d, 16)
            for k in sems:
                moe_sync(sp, sems[k], k == list(sems)[-1])
            sp.wait_ge(s_out, 16 * TT)

        @block.gpsimd
        def _(pool):
            st = Steps(pool, s_pool)
            st(pool.memset(ones[:], 1.0))
            pool.affine_select(out=ident[:], in_=ones[:], compare_op=ALU.is_equal, fill=0.0, base=0,
                               pattern=[[-1, P]], channel_multiplier=1).then_inc(s_const, 1)
            pool.memset(mean_w[:], 1.0 / FF).then_inc(s_const, 1)
            pool.memset(eps_c[:], EPS).then_inc(s_const, 1)
            st(pool.memset(ones16[:], 1.0))
            pool.affine_select(out=before[:], in_=ones16[:], compare_op=ALU.is_gt, fill=0.0, base=0,
                               pattern=[[1, P]], channel_multiplier=-1).then_inc(s_const, 1)
            st(pool.memset(e_lt[:], 1.0))
            pool.affine_select(out=e_lt[:], in_=e_lt[:], compare_op=ALU.is_gt, fill=0.0, base=0,
                               pattern=[[1, NE], [-1, NE]], channel_multiplier=0).then_inc(s_const, 1)
            io = dict(channel_multiplier=0, allow_small_or_imprecise_dtypes=True)
            pool.iota(first_w[:], pattern=[[-1, NE]], base=NE, **io).then_inc(s_const, 1)
            pool.iota(lo_iota[:], pattern=[[1, P]], base=0, **io).then_inc(s_const, 1)
            pool.iota(tile_iota[:], pattern=[[1, 40]], base=0, **io).then_inc(s_const, 1)
            pool.iota(tcol[:], pattern=[[0, TOPK], [1, TT]], base=0, **io).then_inc(s_const, 1)
            pool.iota(row_id[:], pattern=[[0, 1]], base=0, channel_multiplier=1, allow_small_or_imprecise_dtypes=True).then_inc(s_const, 1)
            pool.wait_ge(s_const, 10)
            st(pool.tensor_copy(ident16[:], ident[:]))
            st(pool.memset(mask_q[:], 0.0))
            pool.affine_select(out=mask_k[:], in_=mask_q[:], compare_op=ALU.is_ge, fill=-BIG, base=0,
                               pattern=[[1, P]], channel_multiplier=-1).then_inc(s_const, 1)
            pool.wait_ge(s_const, 11)
            pool.affine_select(out=mask_q[:], in_=mask_q[:], compare_op=ALU.is_ge, fill=-BIG, base=0,
                               pattern=[[-1, P]], channel_multiplier=1).then_inc(s_const, 1)
            pool.memset(neg_half[:], -0.5).then_inc(s_const, 1)
            st(pool.memset(q6[:].bitcast(F32), 0.0))
            st(pool.memset(k6[:].bitcast(F32), 0.0))
            pool.memset(k6[:, :, MAXSLOT, 0:3], 1.0).then_inc(s_const, 1)
            pool.memset(vaug[:, :, :, VD:VD + 1], 1.0).then_inc(s_const, 1)
            pool.wait_ge(s_const, 15)
            pool.dma_start(brb[:], br.rearrange("(o a) -> o a", o=1).to_broadcast([P, NE])).then_inc(s_bc, 16)
            pool.dma_start(g2b[:], g2.rearrange("(o a) d -> o (a d)", o=1).to_broadcast([P, NE * DIM])).then_inc(s_bc, 16)
            pool.dma_start(be2b[:], be2.rearrange("(o a) d -> o (a d)", o=1).to_broadcast([P, NE * DIM])).then_inc(s_bc, 16)
            pool.wait_ge(s_bc, 48)
            pool.memset(gden[:], 0.0).then_inc(s_const, 1)
            pool.wait_ge(s_colc, 1)
            pool.wait_ge(s_ld_w2, 16)
            for h in range(2):
                pool.tensor_tensor(w2c[:].rearrange("p (a d) -> p a d", d=DIM)[:, 16 * h:16 * h + 16, :],
                                  w2s[:, 4 * h:4 * h + 4].rearrange("p a c d -> p (a c) d"),
                                  cols[:, 16 * h:16 * h + 16, None].to_broadcast([P, 16, DIM]), ALU.mult).then_inc(s_w2g, 1)
            for j, w in enumerate((lq1, lk1, lq2, lk2)):
                pool.dma_start(lam_in[:, j, :], w.rearrange("(o a) -> o a", o=1).to_broadcast([P, HD])).then_inc(s_lam, 16)
            pool.wait_ge(s_lam, 64)
            pool.memset(gpad[:, 0:1], 0.0).then_inc(s_ld_a, 16)
            for k in stages:
                att_gpsimd(pool) if k == "at" else moe_gpsimd(pool, sems[k])

        @block.scalar
        def _(act):
            act.wait_ge(s_const, NCONST)
            for k in stages:
                att_scalar(act) if k == "at" else moe_scalar(act, sems[k])

        @block.tensor
        def _(pe):
            pe.wait_ge(s_ld_w, 16 * 6)
            pe.wait_ge(s_const, NCONST)
            pe.transpose(bank[6][:, 0:96], rows[:], ident[0:96, 0:96]).then_inc(s_cols, 1)
            for n, k in enumerate(stages):
                att_tensor(pe) if k == "at" else moe_tensor(pe, sems[k], n == 0)

        @block.vector
        def _(dve):
            step = Steps(dve, s_dve)
            dve.wait_ge(s_cols, 1)
            dve.tensor_copy(cols[:], bank[6][:, 0:96]).then_inc(s_colc, 1)
            for n, k in enumerate(stages):
                att_vector(dve, step) if k == "at" else moe_vector(dve, sems[k], step, n == 0)


_INS = ['L0_attn_x', 'L0_attn_Wq', 'L0_attn_Wk', 'L0_attn_Wv', 'L0_attn_Wo', 'L0_attn_lq1', 'L0_attn_lk1',
        'L0_attn_lq2', 'L0_attn_lk2', 'L0_ffn_Wr', 'L0_ffn_br', 'L0_ffn_W1', 'L0_ffn_b1', 'L0_ffn_g1',
        'L0_ffn_be1', 'L0_ffn_W2', 'L0_ffn_b2', 'L0_ffn_g2', 'L0_ffn_be2']
STAGES = ("f1", "at", "f2")


def kernel(**inputs):
    import numpy as _np
    import concourse.bacc as _bacc
    from concourse import mybir as _mybir
    from concourse.bass_utils import run_bass_kernel_spmd as _run

    nc = _bacc.Bacc("TRN2", target_bir_lowering=False, num_devices=1)
    arrays, args = {}, []
    for name in _INS:
        a = _np.ascontiguousarray(inputs[name])
        arrays[f"in_{name}_dram"] = a
        args.append(nc.dram_tensor(f"in_{name}_dram", a.shape, _mybir.dt.from_np(a.dtype), kind="ExternalInput").ap())
    args.append(nc.dram_tensor("out_0_dram", (BATCH, SEQ, DIM), F32, kind="ExternalOutput").ap())
    build(nc, *args, stages=STAGES)
    r = _run(nc, [arrays], core_ids=[0])
    return r.results[0]["out_0_dram"]
```

```python
from contextlib import ExitStack
import math

import concourse.bass as bass
from concourse import mybir

F32 = mybir.dt.float32
BF16 = mybir.dt.bfloat16
I32 = mybir.dt.int32
U32 = mybir.dt.uint32
ALU = mybir.AluOpType
ACT = mybir.ActivationFunctionType
X = mybir.AxisListType.X

P = 128
BATCH, SEQ, DIM = 8, 256, 128
TOK = BATCH * SEQ
TT = TOK // P
NE, TOPK, FF = 8, 2, 512
FC = FF // P
SLOT_TILES = TOPK * TOK // P + NE - 1
EPS = 1e-5
BIG = 3.0e38


HEADS, HD, SUB = 8, 8, 16
VD = DIM // HEADS
SLOTS, MAXSLOT = 8, 6
LAMBDA_INIT = 0.8 - 0.6 * math.exp(-0.3 * 6)
GUARD = 2.0 ** 60
FRONT_STEPS, BACK_STEPS = 16, 7


PACK = 8


def experts(eng, eid, n, count):
    v = eng.value_load(eid[0:1, bass.ds(n, 1)], min_val=0, max_val=NE ** PACK - 1)
    return [(v >> (3 * k)) & (NE - 1) for k in range(count)]


class Steps:

    def __init__(self, eng, sem):
        self.eng, self.sem, self.n = eng, sem, 0

    def __call__(self, ins):
        ins.then_inc(self.sem, 1)
        self.n += 1
        self.eng.wait_ge(self.sem, self.n)


class LoopSteps:

    def __init__(self, eng, sem):
        self.eng, self.sem, self.base, self.n = eng, sem, 0, 0

    def start(self, base):
        self.base, self.n = base, 0

    def __call__(self, ins):
        ins.then_inc(self.sem, 1)
        self.n += 1
        self.eng.wait_ge(self.sem, self.base + self.n)


def build(nc, x, Wq, Wk, Wv, Wo, lq1, lk1, lq2, lk2, Wr, br, W1, b1, g1, be1, W2, b2, g2, be2, out, stages=("f1", "at", "f2")):
    with ExitStack() as ctx:
        def sb(name, shape, dt=F32):
            return ctx.enter_context(nc.sbuf_tensor(name, shape, dt))

        def sem(name):
            return ctx.enter_context(nc.semaphore(name))

        bank = [ctx.enter_context(nc.psum_tensor(f"bank{i}", [P, 512], F32)) for i in range(3)]
        quad = ctx.enter_context(nc.psum_tensor("quad", [P, 4, 512], F32))
        bank += [quad[:, i, :] for i in range(4)]
        bank.append(ctx.enter_context(nc.psum_tensor("bank7", [P, 512], F32)))

        xn_dram = nc.dram_tensor("xn_scratch", [TOK, DIM], F32).ap()
        y_dram = nc.dram_tensor("y_scratch", [SLOT_TILES * P, DIM], F32).ap()

        xs = sb("xs", [P, TT, DIM])
        xn = sb("xn", [P, TT, DIM])
        w1s = sb("w1s", [P, NE * FF])
        w2s = sb("w2s", [P, NE, FC, DIM])
        w2c = sb("w2c", [P, NE * FC * DIM])
        wrs = sb("wrs", [P, NE])
        rows = sb("rows", [96, P])
        cols = sb("cols", [P, 96])
        b2row = sb("b2row", [1, NE * DIM])
        b2p = sb("b2p", [P, NE * DIM])
        g2b = sb("g2b", [P, NE * DIM])
        be2b = sb("be2b", [P, NE * DIM])
        brb = sb("brb", [P, NE])
        b1lo = sb("b1lo", [32, P])
        b1hi = sb("b1hi", [32, 3, P], BF16)
        b1p = sb("b1p", [3, NE * FF], BF16)

        ident = sb("ident", [P, P])
        ones = sb("ones", [P, P])
        mean_w = sb("mean_w", [P, P])
        ones16 = sb("ones16", [P, P], BF16)
        before = sb("before", [P, P], BF16)
        eps_c = sb("eps_c", [P, 1])
        e_lt = sb("e_lt", [P, NE, NE])
        first_w = sb("first_w", [P, NE])
        lo_iota = sb("lo_iota", [P, P])
        tile_iota = sb("tile_iota", [P, 48])
        row_id = sb("row_id", [P, 1])

        xnT = sb("xnT", [P, 4, P])
        stats = sb("stats", [P, TT, 6])
        mv = sb("mv", [P, TT, 2])
        sdev = sb("sdev", [P, TT])
        rstd = sb("rstd", [P, TT])
        lg = sb("lg", [P, TT, NE])
        lg2 = sb("lg2", [P, TT, NE])
        eq = sb("eq", [P, TT, NE])
        oh = sb("oh", [P, TOPK, TT, NE])
        m12 = sb("m12", [P, TOPK, TT])
        mw = sb("mw", [P, TT])
        picked = sb("picked", [P, TT, NE], BF16)
        gate = sb("gate", [P, TOPK, TT])
        gden = sb("gden", [P, TT])
        ntile = sb("ntile", [P, NE])
        ntile_i = sb("ntile_i", [P, NE], I32)
        start = sb("start", [P, NE])
        end = sb("end", [P, NE])
        tri = sb("tri", [P, NE, NE])
        rank = sb("rank", [P, TT, NE])
        posf = sb("posf", [P, TOPK * TT])
        posi = sb("posi", [P, TOPK * TT], I32)
        hi_i = sb("hi_i", [P, TOPK * TT], I32)
        hi_f = sb("hi_f", [P, TOPK * TT])
        lo_f = sb("lo_f", [P, TOPK * TT])
        posu = sb("posu", [P, TOPK, TT + 2], U32)
        oh_lo = sb("oh_lo", [P, TOPK * TT, P], BF16)
        oh_hi = sb("oh_hi", [P, TOPK * TT, 2, 40], BF16)
        tcol = sb("tcol", [P, TOPK * TT])
        slot_t = sb("slot_t", [P, 40])
        slot_u = sb("slot_u", [P, 40], U32)
        ecmp = sb("ecmp", [1, 48, NE])
        eidf = sb("eidf", [1, 48])
        epk = sb("epk", [1, 2, 40])
        eid = sb("eid", [1, 40], I32)

        xg = sb("xg", [P, 4, DIM])
        xT = sb("xT", [P, 2, P])
        hh = sb("hh", [P, 2, FF])
        hT = sb("hT", [P, 2, FF])
        st1 = sb("st1", [P, 2, 6])
        mv1 = sb("mv1", [P, 2, 2])
        sd1 = sb("sd1", [P, 2, 1])
        r1 = sb("r1", [P, 2, 1])
        yy = sb("yy", [P, 2, DIM])
        st2 = sb("st2", [P, 2, 6])
        mv2 = sb("mv2", [P, 2, 2])
        sd2 = sb("sd2", [P, 2, 1])
        r2 = sb("r2", [P, 2, 1])
        yn = sb("yn", [P, 2, DIM])
        yo = sb("yo", [P, 2, DIM])
        yg = sb("yg", [P, 2, TOPK, DIM])
        idx = sb("idx", [P, TOPK, 2], U32)

        s_ld_x = sem("s_ld_x")
        s_ld_w = sem("s_ld_w")
        s_ld_w2 = sem("s_ld_w2")
        s_ld_w1 = sem("s_ld_w1")
        s_bc = sem("s_bc")
        s_ld_a = sem("s_ld_a")
        s_lam = sem("s_lam")
        s_const = sem("s_const")
        s_pool = sem("s_pool")
        s_dve = sem("s_dve")
        s_cols = sem("s_cols")
        s_colc = sem("s_colc")
        s_b1 = sem("s_b1")
        s_b1d = sem("s_b1d")
        s_w2g = sem("s_w2g")
        s_mean = sem("s_mean")
        s_w2c = sem("s_w2c")
        s_b2m = sem("s_b2m")
        s_b2c = sem("s_b2c")
        s_out = sem("s_out")

        ident16 = sb("ident16", [P, P], BF16)
        mask_q = sb("mask_q", [P, P], BF16)
        mask_k = sb("mask_k", [P, P], BF16)
        neg_half = sb("neg_half", [P, 32])
        wrow = sb("wrow", [P, 4, DIM])
        wqkvo = sb("wqkvo", [P, 4, DIM])
        lam_in = sb("lam_in", [P, 4, HD])
        lam_p = sb("lam_p", [P, 2, HD])
        lam_s = sb("lam_s", [P, 2])
        lam_e = sb("lam_e", [P, 2])
        neg_lam = sb("neg_lam", [P, 1])
        ast = sb("ast", [P, 2, 6])
        amv = sb("amv", [P, 2, 2])
        ave = sb("ave", [P, 2])
        ars = sb("ars", [P, 2])
        axn = sb("axn", [P, 2, DIM])
        axT = sb("axT", [P, 2 * P])
        qk = sb("qk", [P, 2, 2, DIM])
        part = sb("part", [P, 3, 2, 2 * DIM], BF16)
        q6 = sb("q6", [P, 2 * SUB, SLOTS, HD], BF16)
        k6 = sb("k6", [P, 2 * SUB, SLOTS, HD], BF16)
        vaug = sb("vaug", [P, 2, HEADS, 32])
        oTs = sb("oTs", [P, 2, 2, 2 * P])
        kT = sb("kT", [P, HEADS, 2 * P], BF16)
        qT = sb("qT", [P, HEADS, 2 * P], BF16)
        qmT = sb("qmT", [P, HEADS, 2 * P], BF16)
        mx = sb("mx", [P, 2 * SUB])
        mpart = sb("mpart", [P, 3, 2 * SUB], BF16)
        prob = sb("prob", [P, 2, 2, 3 * P])
        rsum = sb("rsum", [P, 2, SUB])
        ow = sb("ow", [P, 2, SUB, VD])
        od = sb("od", [P, 2, HEADS, VD])
        osq = sb("osq", [P, 2, HEADS, VD])
        oms = sb("oms", [P, 2 * HEADS])
        orr = sb("orr", [P, 2 * HEADS])
        vnew = sb("vnew", [P, 2, DIM])
        oT = sb("oT", [P, 2 * P])
        a_names = ("wT wTc lam lame laml var rs xn xTp xTc proj qkv clamp part kcopy qcopy kTp kTc qTp qTc s smax mparts "
                   "qmTp qmTc st prob o oTv ot msq rms onorm oTp oTc res fstep bstep vc vaug x2").split()
        A = {n: sem(f"at_{n}") for n in a_names} if "at" in stages else {}

        names = ("x_ready mv sd rstd xn xnst xnTp xnTc lgp lg top gexp gate picked rankp pos oh slotp slot eid "
                 "xg0 xg1 xg2 xg3 xTp xTc h relu bn mv1 sq1 hTp hTc A ya mv2 sq2 yn yf yst0 yst1 "
                 "yg0 yg1 idx comb lstep lpool").split()
        sems = {k: {n: sem(f"{k}_{n}") for n in names} for k in stages if k != "at"}
        block = ctx.enter_context(nc.Block())

        NCONST = 16

        def moe_sync(sp, S, last):
            sp.wait_ge(S["xn"], TT)
            sp.dma_start(xn_dram.rearrange("(t p) d -> p t d", p=P), xn[:]).then_inc(S["xnst"], 16)
            def store(n, i, u):
                sp.wait_ge(S["yf"], n + 1)
                sp.dma_start(y_dram[bass.ds(n * P, P), :], yo[:, u, :]).then_inc(S[f"yst{u}"], 16)
            with sp.Fori(0, (SLOT_TILES - 1) // 2) as i:
                for u in range(2):
                    store(i * 2 + u, i, u)
            store(SLOT_TILES - 1, 0, 0)
            if last:
                out_t = out.rearrange("b (u p) d -> (b u) p d", p=P)
                for t in range(TT):
                    sp.wait_ge(S["comb"], t + 1)
                    sp.dma_start(out_t[t], xs[:, t, :]).then_inc(s_out, 16)

        def moe_gpsimd(pool, S):
            pool.wait_ge(S["xnst"], 16)
            pool.wait_ge(S["slot"], 1)

            def gather(n, i, u):
                pool.indirect_dma_start(out=xg[:, u, :], out_offset=None, in_=xn_dram,
                                        in_offset=bass.IndirectOffsetOnAxis(ap=slot_u[:, n:n + 1] if isinstance(n, int) else slot_u[:, bass.ds(n, 1)], axis=0)
                                        ).then_inc(S[f"xg{u}"], 16)

            held = []

            def finish(n, i, u):
                if n % 4 == 0:
                    held[:] = experts(pool, eid, n, min(4, SLOT_TILES - n))
                e = held[n % 4]
                pool.wait_ge(S["yn"], n + 1)
                if not (isinstance(n, int) and n < 2):
                    pool.wait_ge(S[f"yst{u}"], i * 16)
                pool.tensor_tensor(yo[:, u, :], yn[:, u, :], g2b[:, bass.ds(e * DIM, DIM)], ALU.mult).then_inc(S["lpool"], 1)
                pool.wait_ge(S["lpool"], n + 1)
                pool.tensor_tensor(yo[:, u, :], yo[:, u, :], be2b[:, bass.ds(e * DIM, DIM)], ALU.add).then_inc(S["yf"], 1)

            pool.wait_ge(S["eid"], 1)
            for n in range(4):
                gather(n, 0, n)
            for n in range(SLOT_TILES):
                if n + 4 < SLOT_TILES:
                    pool.wait_ge(S["xTp"], n + 1)
                    gather(n + 4, 0, n % 4)
                if n:
                    finish(n - 1, (n - 1) // 2, (n - 1) % 2)
            finish(SLOT_TILES - 1, (SLOT_TILES - 1) // 2, 0)

        def combine_gpsimd(pool, S):
            pool.wait_ge(S["yst0"], 16 * ((SLOT_TILES + 1) // 2))
            pool.wait_ge(S["yst1"], 16 * (SLOT_TILES // 2))
            def turn(b, waited=False):
                if not waited:
                    pool.wait_ge(S["idx"], b + 1)
                for u in range(2):
                    for k in range(TOPK):
                        pool.indirect_dma_start(out=yg[:, u, k, :], out_offset=None, in_=y_dram,
                                                in_offset=bass.IndirectOffsetOnAxis(ap=idx[:, k, u:u + 1], axis=0)
                                                ).then_inc(S[f"yg{u}"], 16)
            return turn

        def moe_scalar(act, S):
            act.wait_ge(S["mv"], TT)
            act.activation(sdev[:], mv[:, :, 1], ACT.Sqrt, bias=eps_c[:]).then_inc(S["sd"], 1)
            for g in range(4):
                act.wait_ge(S["xnTp"], g + 1)
                if g:
                    act.wait_ge(S["lgp"], g)
                act.copy(xnT[:], bank[g % 2][:].rearrange("p (a b) -> p a b", a=4)).then_inc(S["xnTc"], 1)
            act.wait_ge(S["top"], 1)
            act.activation(gden[:], mw[:], ACT.Exp).then_inc(S["gexp"], 1)

            def copy_xT(m, u):
                act.wait_ge(S["xTp"], m + 1)
                if not (isinstance(m, int) and m < 2):
                    act.wait_ge(S["h"], m - 1)
                act.copy(xT[:, u, :], bank[0][:, 0:P]).then_inc(S["xTc"], 1)

            def relu(m, u):
                act.wait_ge(S["h"], m + 1)
                if not (isinstance(m, int) and m < 2):
                    act.wait_ge(S["hTp"], m - 1)
                    act.wait_ge(S["bn"], m - 1)
                act.activation(hh[:, u, :], bank[1 + u][:], ACT.Relu).then_inc(S["relu"], 1)

            def sqrt1(m, u):
                act.wait_ge(S["mv1"], m + 1)
                act.activation(sd1[:, u, :], mv1[:, u, 1:2], ACT.Sqrt, bias=eps_c[:]).then_inc(S["sq1"], 1)

            def sqrt2(m, u):
                act.wait_ge(S["mv2"], m + 1)
                act.activation(sd2[:, u, :], mv2[:, u, 1:2], ACT.Sqrt, bias=eps_c[:]).then_inc(S["sq2"], 1)

            def body(n, u, do_x=True, do_h=True, lag=True):
                act.wait_ge(S["hTp"], n + 1)
                if not (isinstance(n, int) and n < 2):
                    act.wait_ge(S["A"], n - 1)
                act.copy(hT[:, u, :], bank[3 + u][:]).then_inc(S["hTc"], 1)
                if do_x:
                    copy_xT(n + 2, u)
                sqrt1(n, u)
                if do_h:
                    relu(n + 1, 1 - u)
                if lag:
                    sqrt2(n - 1, 1 - u)

            copy_xT(0, 0)
            copy_xT(1, 1)
            relu(0, 0)
            body(0, 0, lag=False)
            body(1, 1)
            with act.Fori(1, (SLOT_TILES - 3) // 2) as i:
                for u in range(2):
                    body(i * 2 + u, u)
            for n in range(SLOT_TILES - 3, SLOT_TILES):
                body(n, n % 2, do_x=n + 2 < SLOT_TILES, do_h=n + 1 < SLOT_TILES)
            sqrt2(SLOT_TILES - 1, (SLOT_TILES - 1) % 2)

        def moe_tensor(pe, S, first):
            pe.wait_ge(s_const, NCONST)
            for g in range(4):
                pe.wait_ge(S["xn"], 4 * g + 4)
                if g >= 2:
                    pe.wait_ge(S["xnTc"], g - 1)
                for j in range(4):
                    last = pe.transpose(bank[g % 2][:, j * P:(j + 1) * P], xn[:, 4 * g + j, :], ident[:])
                last.then_inc(S["xnTp"], 1)
                pe.wait_ge(S["xnTc"], g + 1)
                for j in range(4):
                    t = 4 * g + j
                    last = pe.matmul(bank[2][:, t * NE:(t + 1) * NE], xnT[:, j, :], wrs[:], start=True, stop=True)
                last.then_inc(S["lgp"], 1)
            pe.wait_ge(S["picked"], 1)
            pe.matmul(bank[3][:, 0:NE], before[:], picked[:, 0, :], start=True, stop=True)
            pe.matmul(bank[3][:, NE:TT * NE], before[:], picked[:, 1:TT, :], start=True, stop=False)
            for t in range(TT - 2, -1, -1):
                w = TT - 1 - t
                pe.matmul(bank[3][:, (t + 1) * NE:TT * NE].rearrange("p (a b) -> p a b", b=NE), ones16[:],
                          picked[:, t:t + 1, :].to_broadcast([P, w, NE]), start=False, stop=(t == 0),
                          skip_group_check=(t > 0))
            for t in range(TT):
                last = pe.matmul(bank[4][:, 0:NE], ones16[:], picked[:, t, :], start=(t == 0), stop=(t == TT - 1))
            last.then_inc(S["rankp"], 1)
            for c in range(TOPK * TT):
                if c % 8 == 0:
                    pe.wait_ge(S["oh"], c // 8 + 1)
                last = pe.matmul(bank[5][:, 0:80], oh_lo[:, c, :], oh_hi[:, c, :, :], start=(c == 0), stop=(c == TOPK * TT - 1))
            last.then_inc(S["slotp"], 1)
            pe.wait_ge(S["eid"], 1)
            if first:
                weights_tensor(pe)
                pe.wait_ge(s_ld_w1, 16)
            pe.wait_ge(s_w2c, 2)
            pe.wait_ge(s_b1d, 48)
            pe.wait_ge(s_b2c, 1)

            def turn_x(m, i, q):
                pe.wait_ge(S[f"xg{q}"], i * 16 + 16)
                if not (isinstance(m, int) and m == 0):
                    pe.wait_ge(S["xTc"], m)
                pe.transpose(bank[0][:, 0:P], xg[:, q, :], ident[:]).then_inc(S["xTp"], 1)

            def hidden(m, u, e):
                pe.wait_ge(S["xTc"], m + 1)
                if not (isinstance(m, int) and m < 2):
                    pe.wait_ge(S["relu"], m - 1)
                pe.matmul(bank[1 + u][:], ones16[0:3, :], b1p[:, bass.ds(e * FF, FF)], start=True, stop=False)
                pe.matmul(bank[1 + u][:], xT[:, u, :], w1s[:, bass.ds(e * FF, FF)], start=False, stop=True).then_inc(S["h"], 1)

            def turn_h(n, u):
                pe.wait_ge(S["relu"], n + 1)
                if not (isinstance(n, int) and n == 0):
                    pe.wait_ge(S["hTc"], n)
                for c in range(FC):
                    last = pe.transpose(bank[3 + u][:, c * P:c * P + P], hh[:, u, c * P:(c + 1) * P], ident[:])
                last.then_inc(S["hTp"], 1)

            def second(n, u, e):
                pe.wait_ge(S["hTc"], n + 1)
                if not (isinstance(n, int) and n < 2):
                    pe.wait_ge(S["ya"], n - 1)
                for c in range(FC):
                    last = pe.matmul(bank[5 + u][:, 0:DIM], hT[:, u, c * P:(c + 1) * P],
                                     w2c[:, bass.ds(e * (FC * DIM) + c * DIM, DIM)], start=(c == 0), stop=(c == FC - 1))
                last.then_inc(S["A"], 1)

            def body(n, i, q, e, do_x=True, do_h=True):
                turn_h(n, q % 2)
                if do_x:
                    turn_x(n + 2, i + (q + 2) // 4, (q + 2) % 4)
                if do_h:
                    hidden(n + 1, 1 - q % 2, e[1])
                second(n, q % 2, e[0])

            turn_x(0, 0, 0)
            turn_x(1, 0, 1)
            e = experts(pe, eid, 0, 5)
            hidden(0, 0, e[0])
            for n in range(4):
                body(n, 0, n, e[n:])
            with pe.Fori(1, (SLOT_TILES - 3) // 4) as i:
                e = experts(pe, eid, i * 4, 5)
                for q in range(4):
                    body(i * 4 + q, i, q, e[q:])
            e = experts(pe, eid, SLOT_TILES - 3, 3)
            for n in range(SLOT_TILES - 3, SLOT_TILES):
                body(n, n // 4, n % 4, e[n - SLOT_TILES + 3:], do_x=n + 2 < SLOT_TILES, do_h=n + 1 < SLOT_TILES)

        def moe_vector(dve, S, step, first):
            if first:
                dve.wait_ge(s_ld_x, 16)
            for t in range(TT):
                dve.bn_stats(stats[:, t, :], xs[:, t, :]).then_inc(S["lstep"], 1)
            for t in range(TT):
                dve.wait_ge(S["lstep"], t + 1)
                dve.bn_aggr(mv[:, t, :], stats[:, t, :]).then_inc(S["mv"], 1)
            dve.wait_ge(S["sd"], 1)
            step(dve.reciprocal(rstd[:], sdev[:]))
            for t in range(TT):
                dve.tensor_scalar(xn[:, t, :], xs[:, t, :], mv[:, t, 0:1], rstd[:, t:t + 1],
                                  ALU.subtract, ALU.mult).then_inc(S["xn"], 1)
            dve.wait_ge(S["lgp"], 4)
            dve.wait_ge(s_const, NCONST)
            step(dve.tensor_tensor(lg[:], bank[2][:, 0:TT * NE].rearrange("p (a b) -> p a b", b=NE),
                                   brb[:, None, :].to_broadcast([P, TT, NE]), ALU.add))
            for k in range(TOPK):
                src = lg if k == 0 else lg2
                step(dve.tensor_reduce(m12[:, k, :], src[:], X, ALU.max))
                step(dve.tensor_tensor(eq[:], src[:], m12[:, k, :, None].to_broadcast([P, TT, NE]), ALU.is_equal))
                step(dve.tensor_tensor(eq[:], eq[:], first_w[:, None, :].to_broadcast([P, TT, NE]), ALU.mult))
                step(dve.tensor_reduce(mw[:], eq[:], X, ALU.max))
                step(dve.tensor_tensor(oh[:, k], eq[:], mw[:, :, None].to_broadcast([P, TT, NE]), ALU.is_equal))
                if k == 0:
                    step(dve.scalar_tensor_tensor(lg2[:], oh[:, 0], -BIG, lg[:], ALU.mult, ALU.add))
            dve.tensor_tensor(picked[:], oh[:, 0], oh[:, 1], ALU.add).then_inc(S["picked"], 1)
            dve.tensor_tensor(mw[:], m12[:, 1, :], m12[:, 0, :], ALU.subtract).then_inc(S["top"], 1)
            dve.wait_ge(S["rankp"], 1)
            step(dve.tensor_scalar(ntile_i[:], bank[4][:, 0:NE], float(P - 1), None, ALU.add))
            step(dve.tensor_scalar(ntile_i[:], ntile_i[:], 7, None, ALU.arith_shift_right))
            step(dve.tensor_copy(ntile[:], ntile_i[:]))
            step(dve.tensor_tensor(tri[:], e_lt[:], ntile[:, None, :].to_broadcast([P, NE, NE]), ALU.mult))
            step(dve.tensor_reduce(start[:], tri[:], X, ALU.add))
            step(dve.tensor_tensor(end[:], start[:], ntile[:], ALU.add))
            step(dve.scalar_tensor_tensor(rank[:], start[:, None, :].to_broadcast([P, TT, NE]), float(P),
                                          bank[3][:, 0:TT * NE].rearrange("p (a b) -> p a b", b=NE), ALU.mult, ALU.add))
            for k in range(TOPK):
                step(dve.tensor_tensor(eq[:], oh[:, k], rank[:], ALU.mult))
                step(dve.tensor_reduce(posf[:, k * TT:(k + 1) * TT], eq[:], X, ALU.add))
            step(dve.tensor_copy(posi[:], posf[:]))
            dve.tensor_copy(posu[:, :, 0:TT], posf[:].rearrange("p (k t) -> p k t", k=TOPK)).then_inc(S["pos"], 1)
            step(dve.tensor_scalar(hi_i[:], posi[:], 7, None, ALU.arith_shift_right))
            step(dve.tensor_copy(hi_f[:], hi_i[:]))
            step(dve.scalar_tensor_tensor(lo_f[:], hi_f[:], -float(P), posf[:], ALU.mult, ALU.add))
            for q in range(4):
                c = slice(8 * q, 8 * q + 8)
                step(dve.tensor_tensor(oh_lo[:, c, :], lo_f[:, c, None].to_broadcast([P, 8, P]),
                                       lo_iota[:, None, :].to_broadcast([P, 8, P]), ALU.is_equal))
                step(dve.tensor_tensor(oh_hi[:, c, 1, :], hi_f[:, c, None].to_broadcast([P, 8, 40]),
                                       tile_iota[:, None, 0:40].to_broadcast([P, 8, 40]), ALU.is_equal))
                step(dve.tensor_tensor(oh_hi[:, c, 0, :], oh_hi[:, c, 1, :],
                                       tcol[:, c, None].to_broadcast([P, 8, 40]), ALU.mult))
                dve.tensor_scalar(oh_hi[:, c, 1, :], oh_hi[:, c, 1, :], row_id[:], None, ALU.mult).then_inc(S["oh"], 1)
            step(dve.tensor_tensor(ecmp[:], tile_iota[0:1, :, None].to_broadcast([1, 48, NE]),
                                   end[0:1, None, :].to_broadcast([1, 48, NE]), ALU.is_ge))
            step(dve.tensor_reduce(eidf[:], ecmp[:], X, ALU.add))
            step(dve.tensor_scalar(eidf[:], eidf[:], float(NE - 1), None, ALU.min))
            src = eidf[:, PACK - 1:PACK + 39]
            for j in range(PACK - 2, -1, -1):
                dst = eid if j == 0 else epk[:, j % 2]
                ins = dve.scalar_tensor_tensor(dst[:], src, float(NE), eidf[:, j:j + 40], ALU.mult, ALU.add)
                if j:
                    step(ins)
                src = dst
            ins.then_inc(S["eid"], 1)
            dve.wait_ge(S["slotp"], 1)
            step(dve.tensor_copy(slot_t[:], bank[5][:, 40:80]))
            dve.scalar_tensor_tensor(slot_u[:], bank[5][:, 0:40], float(P), slot_t[:], ALU.mult, ALU.add).then_inc(S["slot"], 1)
            dve.wait_ge(S["gexp"], 1)
            step(dve.tensor_scalar(m12[:, 0, :], gden[:], 2.0, 2.0, ALU.mult, ALU.add))
            step(dve.reciprocal(gate[:, 0, :], m12[:, 0, :]))
            dve.tensor_tensor(gate[:, 1, :], gate[:, 0, :], gden[:], ALU.mult).then_inc(S["gate"], 1)
            if first:
                weights_vector(dve, step)

            ls = LoopSteps(dve, S["lstep"])
            PER = 4

            def stats1(m, u):
                dve.wait_ge(S["relu"], m + 1)
                if not (isinstance(m, int) and m < 2):
                    dve.wait_ge(S["sq1"], m - 1)
                dve.bn_stats(st1[:, u, :], hh[:, u, :]).then_inc(S["bn"], 1)
                dve.wait_ge(S["bn"], m + 1)
                dve.memset(hold[:, 0:1], 0.0)
                dve.bn_aggr(mv1[:, u, :], st1[:, u, :]).then_inc(S["mv1"], 1)

            def y_part(m, u, e):
                ls.start(m * PER + TT)
                dve.wait_ge(S["sq1"], m + 1)
                ls(dve.reciprocal(r1[:, u, :], sd1[:, u, :]))
                dve.wait_ge(S["A"], m + 1)
                dve.scalar_tensor_tensor(yy[:, u, :], bank[5 + u][:, 0:DIM], r1[:, u, :],
                                         b2p[:, bass.ds(e * DIM, DIM)], ALU.mult, ALU.add).then_inc(S["ya"], 1)
                dve.wait_ge(S["ya"], m + 1)
                ls(dve.tensor_scalar(yy[:, u, :], yy[:, u, :], 0.0, None, ALU.max))
                dve.bn_stats(st2[:, u, :], yy[:, u, :]).then_inc(S["lstep"], 1)
                dve.wait_ge(S["lstep"], m * PER + TT + 3)
                dve.memset(hold[:, 1:2], 0.0)
                dve.bn_aggr(mv2[:, u, :], st2[:, u, :]).then_inc(S["mv2"], 1)

            def y_norm(m, u):
                ls.base, ls.n = m * PER + TT, 3
                dve.wait_ge(S["sq2"], m + 1)
                ls(dve.reciprocal(r2[:, u, :], sd2[:, u, :]))
                if not (isinstance(m, int) and m < 2):
                    dve.wait_ge(S["yf"], m - 1)
                dve.tensor_scalar(yn[:, u, :], yy[:, u, :], mv2[:, u, 0:1], r2[:, u, :],
                                  ALU.subtract, ALU.mult).then_inc(S["yn"], 1)

            def body(n, u, e=None, do_h=True):
                if e is not None:
                    y_part(n - 1, 1 - u, e)
                if do_h:
                    stats1(n + 1, 1 - u)
                if e is not None:
                    y_norm(n - 1, 1 - u)

            stats1(0, 0)
            e = experts(dve, eid, 0, 3)
            body(0, 0)
            for n in range(1, 4):
                body(n, n % 2, e[n - 1])
            with dve.Fori(1, (SLOT_TILES - 3) // 4) as i:
                e = experts(dve, eid, i * 4 - 1, 4)
                for q in range(4):
                    body(i * 4 + q, q % 2, e[q])
            e = experts(dve, eid, SLOT_TILES - 4, 4)
            for n in range(SLOT_TILES - 3, SLOT_TILES):
                body(n, n % 2, e[n - SLOT_TILES + 3], do_h=n + 1 < SLOT_TILES)
            y_part(SLOT_TILES - 1, 0, e[3])
            y_norm(SLOT_TILES - 1, 0)

        def combine_vector(dve, S, base):
            def next_index(b):
                dve.tensor_copy(idx[:], posu[:, :, bass.ds(b * 2, 2)]).then_inc(S["idx"], 1)

            def turn(b):
                for k in range(TOPK):
                    for u in range(2):
                        if k == 0:
                            dve.wait_ge(S[f"yg{u}"], b * 32 + 32)
                        else:
                            dve.wait_ge(S["lstep"], b * 2 + (base + u + 1))
                        ins = dve.scalar_tensor_tensor(
                            xs[:, bass.ds(b * 2 + u, 1), :].rearrange("p a e -> p (a e)"), yg[:, u, k, :],
                            gate[:, k:k + 1, bass.ds(b * 2 + u, 1)].rearrange("p a e -> p (a e)"),
                            xs[:, bass.ds(b * 2 + u, 1), :].rearrange("p a e -> p (a e)"), ALU.mult, ALU.add)
                        ins.then_inc(S["lstep" if k == 0 else "comb"], 1)
                dve.wait_ge(S["comb"], b * 2 + 2)
            return next_index, turn

        def turns(eng, turn):
            turn(0, True, False)
            with eng.Fori(1, BATCH) as t:
                turn(t, True, True)
            turn(BATCH, False, True)

        def att_gpsimd(pool, gather):
            def turn(t, front, back):
                if front:
                    pool.wait_ge(A["var"], t + 1)
                    pool.tensor_tensor(ars[:], ave[:], neg_half[:, 0:2], ALU.pow).then_inc(A["rs"], 1)
                    gather(t + 1, waited=True)
                if back:
                    pool.wait_ge(A["msq"], t)
                    pool.tensor_tensor(orr[:], oms[:], neg_half[:, 0:2 * HEADS], ALU.pow).then_inc(A["rms"], 1)
            gather(0)
            turns(pool, turn)

        def att_scalar(act):
            act.wait_ge(A["wT"], 1)
            act.copy(wqkvo[:].rearrange("p a b -> p (a b)"), bank[7][:]).then_inc(A["wTc"], 1)
            act.wait_ge(A["lam"], 1)
            act.activation(lam_e[:], lam_s[:], ACT.Exp).then_inc(A["lame"], 1)

            def turn(t, front, back):
                c = t - 1
                if back:
                    for u, bk in enumerate((2, 0)):
                        act.wait_ge(A["qmTp"], c * 2 + u + 1)
                        act.copy(qmT[:, :, u * P:u * P + P], bank[bk][:].bitcast(BF16).rearrange("p (a e) -> p a e", e=P)).then_inc(A["qmTc"], 1)
                for g in range(HEADS):
                    if back:
                        act.wait_ge(A["st"], c * 8 + g + 1)
                        if g >= 2:
                            act.wait_ge(A["o"], c * 8 + g - 1)
                        act.activation(prob[:, g % 2], quad[:, g % 2 * 2:g % 2 * 2 + 2, 0:3 * P], ACT.Exp).then_inc(A["prob"], 1)
                    if front and g == 1:
                        act.wait_ge(A["xTp"], t + 1)
                        act.copy(axT[:], bank[1][:, 0:2 * P]).then_inc(A["xTc"], 1)
                    if front and g in (3, 4):
                        u = g - 3
                        act.wait_ge(A["proj"], t * 2 + u + 1)
                        act.activation(qk[:, 0, u, :], bank[1][:, 0:DIM], ACT.Copy, scale=HD ** -0.5)
                        act.copy(qk[:, 1, u, :], bank[1][:, DIM:2 * DIM]).then_inc(A["qkv"], 1)
                        if u == 0:
                            act.copy(vnew[:, 0, :], bank[1][:, 2 * DIM:3 * DIM]).then_inc(A["vc"], 1)
                        else:
                            act.copy(vnew[:, 1, :], bank[1][:, 2 * DIM:3 * DIM]).then_inc(A["vc"], 1)
                    if back and g in (5, 7):
                        act.wait_ge(A["o"], c * 8 + (4 if g == 5 else 8))
                        act.copy(oTs[:, (g - 5) // 2].rearrange("p a e -> p (a e)"), bank[7 if g == 5 else 0][:]).then_inc(A["oTv"], 1)
                if front:
                    for u in range(2):
                        act.wait_ge(A["kTp"], t * 2 + u + 1)
                        act.copy(kT[:, :, u * P:u * P + P], quad[:, u, :].bitcast(BF16).rearrange("p (a e) -> p a e", e=P)).then_inc(A["kTc"], 1)
                    for u in range(2):
                        act.wait_ge(A["qTp"], t * 2 + u + 1)
                        act.copy(qT[:, :, u * P:u * P + P], quad[:, 2 + u, :].bitcast(BF16).rearrange("p (a e) -> p a e", e=P)).then_inc(A["qTc"], 1)
                if back:
                    act.wait_ge(A["oTp"], c + 1)
                    act.copy(oT[:], bank[1][:, 0:2 * P]).then_inc(A["oTc"], 1)
            turns(act, turn)

        def att_tensor(pe):
            pe.wait_ge(s_ld_a, 80)
            for j in range(4):
                last = pe.transpose(bank[7][:, j * P:(j + 1) * P], wrow[:, j, :], ident[:])
            last.then_inc(A["wT"], 1)
            pe.wait_ge(A["wTc"], 1)

            def turn8(src, u, dst):
                for hp in range(HEADS):
                    last = pe.transpose(dst.bitcast(BF16)[:, hp * P:hp * P + P],
                                        src[:, u * SUB + 2 * hp:u * SUB + 2 * hp + 2].rearrange("p a s e -> p (a s e)"), ident16[:])
                return last

            def scores(b, n):
                u, h0, per = (0, 8 * n, 4) if n < 2 else (1, 4 * (n - 2), 2)
                w = (u + 1) * P
                if n >= 2:
                    pe.wait_ge(A["smax"], b * 6 + n - 1)
                for a in range(per):
                    hs = [(h, slice(64 * (h % 2), 64 * (h % 2) + MAXSLOT * HD), quad[:, n % 2 * 2 + h % 2, a * w:(a + 1) * w])
                          for h in (h0 + 2 * a, h0 + 2 * a + 1)]
                    if u:
                        for h, r, o in hs:
                            pe.matmul(o[:, 0:P], qT[r, h // 2, P:2 * P], kT[r, h // 2, 0:P], start=True, stop=True)
                    for h, r, o in hs:
                        pe.matmul(o[:, w - P:w], ident16[:], mask_q[:], start=True, stop=False)
                    for h, r, o in hs:
                        last = pe.matmul(o[:, w - P:w], qT[r, h // 2, u * P:u * P + P], kT[r, h // 2, u * P:u * P + P],
                                         start=False, stop=True)
                last.then_inc(A["s"], 1)

            def scores_t(b, g):
                if g >= 2:
                    pe.wait_ge(A["prob"], b * 8 + g - 1)
                hs = [(slice(64 * p, 64 * p + 64), quad[:, g % 2 * 2 + p, :]) for p in range(2)]
                for r, o in hs:
                    pe.matmul(o[:, P:2 * P], kT[r, g, 0:P], qmT[r, g, P:2 * P], start=True, stop=True)
                for r, o in hs:
                    pe.matmul(o.rearrange("p (a e) -> p a e", e=2 * P)[:, :, 0:P], ident16[:],
                              mask_k[:, None, :].to_broadcast([P, 2, P]), start=True, stop=False)
                for r, o in hs:
                    pe.matmul(o[:, 0:P], kT[r, g, 0:P], qmT[r, g, 0:P], start=False, stop=False)
                for r, o in hs:
                    last = pe.matmul(o[:, 2 * P:3 * P], kT[r, g, P:2 * P], qmT[r, g, P:2 * P], start=False, stop=True)
                last.then_inc(A["st"], 1)

            def values(b, g):
                pe.wait_ge(A["prob"], b * 8 + g + 1)
                v0, v1 = (vaug[:, u, g, :] for u in range(2))
                o = bank[7 if g < 4 else 0][32 * (g % 4):32 * (g % 4) + 32, :].rearrange("p (a e) -> p a e", a=2)
                pr = prob[:, g % 2]
                pe.matmul(o[:, :, 0:P], v0, pr[:, :, 0:P], start=True, stop=True, tile_position=(0, 32 * (g % 4)))
                pe.matmul(o[:, :, P:2 * P], v0, pr[:, :, P:2 * P], start=True, stop=False, tile_position=(0, 32 * (g % 4)))
                pe.matmul(o[:, :, P:2 * P], v1, pr[:, :, 2 * P:3 * P], start=False, stop=True,
                          tile_position=(0, 32 * (g % 4))).then_inc(A["o"], 1)

            def turn_o(b):
                pe.wait_ge(A["oTv"], b * 2 + 2)
                for u, bk in enumerate((7, 0)):
                    for r in range(4):
                        last = pe.transpose(bank[bk][:, r * P:r * P + P], oTs[:, r // 2, r % 2, u * P:u * P + P], ident[:])
                last.then_inc(A["ot"], 1)

            def turn(t, front, back):
                c = t - 1
                if back:
                    pe.wait_ge(A["mparts"], c + 1)
                    turn8(q6, 0, bank[2][:]).then_inc(A["qmTp"], 1)
                    turn8(q6, 1, bank[0][:]).then_inc(A["qmTp"], 1)
                    pe.wait_ge(A["qmTc"], c * 2 + 2)
                    pe.wait_ge(A["vaug"], c + 1)
                for g in range(HEADS + 1):
                    if back and g < HEADS:
                        scores_t(c, g)
                    if back and g:
                        values(c, g - 1)
                    if front and g == 0:
                        pe.wait_ge(A["xn"], t + 1)
                        for u in range(2):
                            last = pe.transpose(bank[1][:, u * P:u * P + P], axn[:, u, :], ident[:])
                        last.then_inc(A["xTp"], 1)
                    if front and g in (2, 3):
                        u = g - 2
                        if u == 0:
                            pe.wait_ge(A["xTc"], t + 1)
                        else:
                            pe.wait_ge(A["vc"], t * 2 + 1)
                        pe.matmul(bank[1][:, 0:3 * DIM], axT[:, u * P:u * P + P], wqkvo[:, 0:3, :], start=True, stop=True).then_inc(A["proj"], 1)
                if front:
                    pe.wait_ge(A["kcopy"], t + 1)
                if back:
                    turn_o(c)
                if front:
                    for u in range(2):
                        turn8(k6, u, quad[:, u, :]).then_inc(A["kTp"], 1)
                    for u in range(2):
                        turn8(q6, u, quad[:, 2 + u, :]).then_inc(A["qTp"], 1)
                    pe.wait_ge(A["qTc"], t * 2 + 2)
                    for n in range(3):
                        scores(t, n)
                if back:
                    pe.wait_ge(A["onorm"], c + 1)
                    for u in range(2):
                        last = pe.transpose(bank[1][:, u * P:u * P + P], od[:, u].rearrange("p a e -> p (a e)"), ident[:])
                    last.then_inc(A["oTp"], 1)
                if front:
                    scores(t, 3)
                    scores(t, 4)
                if back:
                    pe.wait_ge(A["oTc"], c + 1)
                    for u in range(2):
                        last = pe.matmul(bank[1][:, (2 + u) * P:(3 + u) * P], oT[:, u * P:u * P + P], wqkvo[:, 3, :], start=True, stop=True)
                    last.then_inc(A["res"], 1)
                if front:
                    scores(t, 5)
            turns(pe, turn)

        def att_vector(dve, step, next_index, combine):
            dve.wait_ge(s_ld_a, 80)
            step(dve.tensor_tensor(lam_p[:], lam_in[:, 0:4:2, :], lam_in[:, 1:4:2, :], ALU.mult))
            dve.tensor_reduce(lam_s[:], lam_p[:], X, ALU.add).then_inc(A["lam"], 1)
            dve.wait_ge(A["lame"], 1)
            step(dve.tensor_tensor(neg_lam[:], lam_e[:, 1:2], lam_e[:, 0:1], ALU.subtract))
            step(dve.tensor_scalar(neg_lam[:], neg_lam[:], -LAMBDA_INIT, None, ALU.add))
            dve.wait_ge(A["wTc"], 1)
            fs, bs = LoopSteps(dve, A["fstep"]), LoopSteps(dve, A["bstep"])

            def norm(b):
                for u in range(2):
                    dve.bn_stats(ast[:, u, :], xs[:, bass.ds(b * 2 + u, 1), :]).then_inc(A["fstep"], 1)
                    fs.n += 1
                dve.wait_ge(A["fstep"], fs.base + fs.n)
                dve.memset(hold[:, 0:1], 0.0)
                for u in range(2):
                    dve.bn_aggr(amv[:, u, :], ast[:, u, :]).then_inc(A["fstep"], 1)
                    fs.n += 1
                dve.wait_ge(A["fstep"], fs.base + fs.n)
                dve.tensor_scalar(ave[:], amv[:, :, 1], EPS, None, ALU.add).then_inc(A["var"], 1)
                dve.wait_ge(A["rs"], b + 1)
                for u in range(2):
                    last = dve.tensor_scalar(axn[:, u, :], xs[:, bass.ds(b * 2 + u, 1), :].rearrange("p a e -> p (a e)"),
                                             amv[:, u, 0:1], ars[:, u:u + 1], ALU.subtract, ALU.mult)
                last.then_inc(A["xn"], 1)

            def split(b, back):
                dve.wait_ge(A["qkv"], b * 2 + 2)
                qk2 = qk[:].rearrange("p a u e -> p a (u e)")
                fs(dve.tensor_scalar(qk2, qk2, GUARD, -GUARD, ALU.min, ALU.max))
                for j in range(3):
                    fs(dve.tensor_copy(part[:, j], qk2))
                    if j < 2:
                        fs(dve.tensor_tensor(qk2, qk2, part[:, j], ALU.subtract))
                for dst, a, j, at in ((k6, 1, 0, slice(0, 4, 3)), (k6, 1, 0, slice(5, 6)), (k6, 1, 1, slice(1, 5, 3)), (k6, 1, 2, slice(2, 3)),
                                      (q6, 0, 0, slice(0, 3)), (q6, 0, 1, slice(3, 5)), (q6, 0, 2, slice(5, 6))):
                    n = len(range(*at.indices(SLOTS)))
                    last = dve.tensor_copy(dst[:, :, at, :], part[:, j, a, :].rearrange("p (a e) -> p a e", e=HD)[:, :, None, :]
                                           .to_broadcast([P, 2 * SUB, n, HD]))
                last.then_inc(A["kcopy"], 1)

            def row_max(b, n):
                u, h0, per = (0, 8 * n, 4) if n < 2 else (1, 4 * (n - 2), 2)
                dve.wait_ge(A["s"], b * 6 + n + 1)
                c = u * SUB + h0
                dve.tensor_reduce(mx[:, c:c + 2 * per].rearrange("p (a q) -> p q a", q=2),
                                  quad[:, n % 2 * 2:n % 2 * 2 + 2, :].rearrange("p q (a e) -> p q a e", a=per), X, ALU.max
                                  ).then_inc(A["smax"], 1)

            def max_parts(b):
                dve.wait_ge(A["smax"], b * 6 + 6)
                fs(dve.tensor_scalar(mx[:], mx[:], -1.0, None, ALU.mult))
                for j in range(3):
                    fs(dve.tensor_copy(mpart[:, j, :], mx[:]))
                    if j < 2:
                        fs(dve.tensor_tensor(mx[:], mx[:], mpart[:, j, :], ALU.subtract))
                dve.tensor_copy(q6[:, :, MAXSLOT, 0:3], mpart[:].rearrange("p j a -> p a j")).then_inc(A["mparts"], 1)

            def outputs(c):
                dve.wait_ge(A["ot"], c + 1)
                obs = [bank[bk][:].rearrange("p (r e) -> p r e", e=32) for bk in (7, 0)]
                for u in range(2):
                    last = dve.reciprocal(rsum[:, u, :], obs[u][:, :, VD])
                bs(last)
                second = rsum[:].rearrange("p u (j s g) -> p (u j) s g", s=2, g=4)[:, :, 1, :]
                bs(dve.tensor_scalar(second, second, neg_lam[:], None, ALU.mult))
                for u in range(2):
                    last = dve.tensor_tensor(ow[:, u], obs[u][:, :, 0:VD], rsum[:, u, :, None].to_broadcast([P, SUB, VD]), ALU.mult)
                bs(last)
                owv = ow[:].rearrange("p u (j s g) e -> p (u j) s (g e)", s=2, g=4)
                bs(dve.tensor_tensor(od[:].rearrange("p u (j g) e -> p (u j) (g e)", g=4), owv[:, :, 0, :], owv[:, :, 1, :], ALU.add))
                bs(dve.tensor_tensor(osv, odv, odv, ALU.mult))
                bs(dve.tensor_reduce(oms[:], osv, X, ALU.add))
                dve.tensor_scalar(oms[:], oms[:], 1.0 / VD, EPS, ALU.mult, ALU.add).then_inc(A["msq"], 1)

            odv = od[:].rearrange("p u a e -> p (u a) e")
            osv = osq[:].rearrange("p u a e -> p (u a) e")

            def rms(c):
                dve.wait_ge(A["rms"], c + 1)
                bs(dve.tensor_scalar(orr[:], orr[:], 1.0 - LAMBDA_INIT, None, ALU.mult))
                dve.tensor_tensor(odv, odv, orr[:, :, None].to_broadcast([P, 2 * HEADS, VD]), ALU.mult).then_inc(A["onorm"], 1)

            def residual(c):
                dve.wait_ge(A["res"], c + 1)
                x2 = xs[:, bass.ds(c * 2, 2), :]
                dve.tensor_tensor(x2, x2, bank[1][:, 2 * P:4 * P].rearrange("p (a e) -> p a e", e=DIM), ALU.add).then_inc(A["x2"], 1)

            def turn(t, front, back):
                c = t - 1
                fs.start(t * FRONT_STEPS)
                bs.start(c * BACK_STEPS)
                if front:
                    combine(t)
                    next_index(t + 1)
                    norm(t)
                    split(t, back)
                if back:
                    outputs(c)
                if front:
                    dve.wait_ge(A["vc"], t * 2 + 2)
                    dve.tensor_copy(vaug[:, :, :, 0:VD], vnew[:].rearrange("p u (a e) -> p u a e", e=VD)).then_inc(A["vaug"], 1)
                    row_max(t, 0)
                    row_max(t, 1)
                if back:
                    rms(c)
                if front:
                    row_max(t, 2)
                    row_max(t, 3)
                    row_max(t, 4)
                if back:
                    residual(c)
                if front:
                    row_max(t, 5)
                    max_parts(t)
                    assert fs.n == FRONT_STEPS, fs.n
                if back:
                    assert bs.n == BACK_STEPS, bs.n

            next_index(0)
            turns(dve, turn)
            dve.wait_ge(A["x2"], BATCH)
            for u in range(2):
                dve.wait_ge(sems["f1"][f"yg{u}"], 32 * (BATCH + 1))

        def weights_vector(dve, step):
            dve.wait_ge(s_ld_w, 16 * 6)
            step(dve.tensor_copy(b1hi[:, 0, :], b1s[:]))
            step(dve.tensor_tensor(b1lo[:], b1s[:], b1hi[:, 0, :], ALU.subtract))
            step(dve.tensor_copy(b1hi[:, 1, :], b1lo[:]))
            step(dve.tensor_tensor(b1lo[:], b1lo[:], b1hi[:, 1, :], ALU.subtract))
            dve.tensor_copy(b1hi[:, 2, :], b1lo[:]).then_inc(s_b1, 1)
            w2cv = w2c[:].rearrange("p (a c d) -> p a c d", a=NE, c=FC)
            dve.wait_ge(s_b2m, 1)
            for h in range(2):
                step(dve.tensor_copy(b2p[:, 512 * h:512 * h + 512], bank[6 + h][:]))
            dve.engine_nop().then_inc(s_b2c, 1) if False else dve.sem_inc(s_b2c, 1)
            dve.wait_ge(s_w2g, 2)
            for h in range(2):
                dve.wait_ge(s_mean, h + 1)
                for a in range(4):
                    e = 4 * h + a
                    ins = dve.tensor_tensor(w2cv[:, e], w2cv[:, e],
                                            bank[1 + h][:, None, a * DIM:(a + 1) * DIM].to_broadcast([P, FC, DIM]), ALU.subtract)
                    if a < 3:
                        step(ins)
                ins.then_inc(s_w2c, 1)

        def weights_tensor(pe):
            pe.wait_ge(s_colc, 1)
            pe.wait_ge(s_ld_w2, 16)
            for h in range(2):
                for a in range(4):
                    e = 4 * h + a
                    o = bank[6 + h][:, a * DIM:(a + 1) * DIM]
                    for c in range(FC):
                        j = 32 + e * FC + c
                        pe.matmul(o, cols[:, j:j + 1].to_broadcast([P, P]), w2s[:, e, c, :], start=(c == 0), stop=False)
                    last = pe.matmul(o, ones[0:1, :], b2row[:, e * DIM:(e + 1) * DIM], start=False, stop=True)
            last.then_inc(s_b2m, 1)
            w2cv = w2c[:].rearrange("p (a c d) -> p a c d", a=NE, c=FC)
            for h in range(2):
                pe.wait_ge(s_w2g, h + 1)
                for c in range(FC):
                    last = pe.matmul(bank[1 + h][:].rearrange("p (a d) -> p a d", d=DIM), mean_w[:],
                                     w2cv[:, 4 * h:4 * h + 4, c, :], start=(c == 0), stop=(c == FC - 1))
                last.then_inc(s_mean, 1)

        b1s = sb("b1s", [32, P])
        hold = sb("hold", [1, 2])
        gpad = sb("gpad", [1, 2])

        @block.sync
        def _(sp):
            sp.dma_start(xs[:], x.rearrange("b (u p) d -> p (b u) d", p=P)).then_inc(s_ld_x, 16)
            sp.dma_start(wrs[:], Wr).then_inc(s_ld_w, 16)
            sp.dma_start(rows[0:32, :], g1.rearrange("a (c p) -> (a c) p", p=P)).then_inc(s_ld_w, 16)
            sp.dma_start(rows[32:64, :], be1.rearrange("a (c p) -> (a c) p", p=P)).then_inc(s_ld_w, 16)
            sp.dma_start(rows[64:96, :], b1.rearrange("a (c p) -> (a c) p", p=P)).then_inc(s_ld_w, 16)
            sp.dma_start(b1s[:], b1.rearrange("a (c p) -> (a c) p", p=P)).then_inc(s_ld_w, 16)
            sp.dma_start(b2row[:], b2.rearrange("(o a) d -> o (a d)", o=1)).then_inc(s_ld_w, 16)
            sp.dma_start(w2s[:].rearrange("p a c d -> p (a c) d"), W2.rearrange("a (c p) d -> p (a c) d", p=P)).then_inc(s_ld_w2, 16)
            sp.dma_start(w1s[:].rearrange("p (a f) -> p a f", a=NE), W1.rearrange("a p f -> p a f")).then_inc(s_ld_w1, 16)
            for j, w in enumerate((Wq, Wk, Wv, Wo)):
                sp.dma_start(wrow[:, j, :], w).then_inc(s_ld_a, 16)
            sp.wait_ge(s_b1, 1)
            for j in range(3):
                sp.dma_start(b1p[j:j + 1, :], b1hi[:, j, :]).then_inc(s_b1d, 16)
            for k in sems:
                moe_sync(sp, sems[k], k == list(sems)[-1])
            sp.wait_ge(s_out, 16 * TT)

        @block.gpsimd
        def _(pool):
            st = Steps(pool, s_pool)
            st(pool.memset(ones[:], 1.0))
            pool.affine_select(out=ident[:], in_=ones[:], compare_op=ALU.is_equal, fill=0.0, base=0,
                               pattern=[[-1, P]], channel_multiplier=1).then_inc(s_const, 1)
            pool.memset(mean_w[:], 1.0 / FF).then_inc(s_const, 1)
            pool.memset(eps_c[:], EPS).then_inc(s_const, 1)
            st(pool.memset(ones16[:], 1.0))
            pool.affine_select(out=before[:], in_=ones16[:], compare_op=ALU.is_gt, fill=0.0, base=0,
                               pattern=[[1, P]], channel_multiplier=-1).then_inc(s_const, 1)
            st(pool.memset(e_lt[:], 1.0))
            pool.affine_select(out=e_lt[:], in_=e_lt[:], compare_op=ALU.is_gt, fill=0.0, base=0,
                               pattern=[[1, NE], [-1, NE]], channel_multiplier=0).then_inc(s_const, 1)
            io = dict(channel_multiplier=0, allow_small_or_imprecise_dtypes=True)
            pool.iota(first_w[:], pattern=[[-1, NE]], base=NE, **io).then_inc(s_const, 1)
            pool.iota(lo_iota[:], pattern=[[1, P]], base=0, **io).then_inc(s_const, 1)
            pool.iota(tile_iota[:], pattern=[[1, 48]], base=0, **io).then_inc(s_const, 1)
            pool.iota(tcol[:], pattern=[[0, TOPK], [1, TT]], base=0, **io).then_inc(s_const, 1)
            pool.iota(row_id[:], pattern=[[0, 1]], base=0, channel_multiplier=1, allow_small_or_imprecise_dtypes=True).then_inc(s_const, 1)
            pool.wait_ge(s_const, 10)
            st(pool.tensor_copy(ident16[:], ident[:]))
            st(pool.memset(mask_q[:], 0.0))
            pool.affine_select(out=mask_k[:], in_=mask_q[:], compare_op=ALU.is_ge, fill=-BIG, base=0,
                               pattern=[[1, P]], channel_multiplier=-1).then_inc(s_const, 1)
            pool.wait_ge(s_const, 11)
            pool.affine_select(out=mask_q[:], in_=mask_q[:], compare_op=ALU.is_ge, fill=-BIG, base=0,
                               pattern=[[-1, P]], channel_multiplier=1).then_inc(s_const, 1)
            st(pool.memset(posu[:], 0))
            pool.memset(neg_half[:], -0.5).then_inc(s_const, 1)
            st(pool.memset(q6[:].bitcast(F32), 0.0))
            st(pool.memset(k6[:].bitcast(F32), 0.0))
            pool.memset(k6[:, :, MAXSLOT, 0:3], 1.0).then_inc(s_const, 1)
            st(pool.memset(vaug[:], 0.0))
            pool.memset(vaug[:, :, :, VD:VD + 1], 1.0).then_inc(s_const, 1)
            pool.wait_ge(s_const, 15)
            pool.dma_start(brb[:], br.rearrange("(o a) -> o a", o=1).to_broadcast([P, NE])).then_inc(s_bc, 16)
            pool.dma_start(g2b[:], g2.rearrange("(o a) d -> o (a d)", o=1).to_broadcast([P, NE * DIM])).then_inc(s_bc, 16)
            pool.dma_start(be2b[:], be2.rearrange("(o a) d -> o (a d)", o=1).to_broadcast([P, NE * DIM])).then_inc(s_bc, 16)
            pool.wait_ge(s_bc, 48)
            pool.memset(gden[:], 0.0).then_inc(s_const, 1)
            pool.wait_ge(s_colc, 1)
            pool.wait_ge(s_ld_w2, 16)
            for h in range(2):
                pool.tensor_tensor(w2c[:].rearrange("p (a d) -> p a d", d=DIM)[:, 16 * h:16 * h + 16, :],
                                  w2s[:, 4 * h:4 * h + 4].rearrange("p a c d -> p (a c) d"),
                                  cols[:, 16 * h:16 * h + 16, None].to_broadcast([P, 16, DIM]), ALU.mult).then_inc(s_w2g, 1)
            for j, w in enumerate((lq1, lk1, lq2, lk2)):
                pool.dma_start(lam_in[:, j, :], w.rearrange("(o a) -> o a", o=1).to_broadcast([P, HD])).then_inc(s_lam, 16)
            pool.wait_ge(s_lam, 64)
            pool.memset(gpad[:, 0:1], 0.0).then_inc(s_ld_a, 16)
            moe_gpsimd(pool, sems["f1"])
            att_gpsimd(pool, combine_gpsimd(pool, sems["f1"]))
            moe_gpsimd(pool, sems["f2"])
            gather = combine_gpsimd(pool, sems["f2"])
            for b in range(BATCH):
                gather(b)

        @block.scalar
        def _(act):
            act.wait_ge(s_const, NCONST)
            for k in stages:
                att_scalar(act) if k == "at" else moe_scalar(act, sems[k])

        @block.tensor
        def _(pe):
            pe.wait_ge(s_ld_w, 16 * 6)
            pe.wait_ge(s_const, NCONST)
            pe.transpose(bank[6][:, 0:96], rows[:], ident[0:96, 0:96]).then_inc(s_cols, 1)
            for n, k in enumerate(stages):
                att_tensor(pe) if k == "at" else moe_tensor(pe, sems[k], n == 0)

        @block.vector
        def _(dve):
            step = Steps(dve, s_dve)
            dve.wait_ge(s_cols, 1)
            dve.tensor_copy(cols[:], bank[6][:, 0:96]).then_inc(s_colc, 1)
            base = TT + 4 * SLOT_TILES
            moe_vector(dve, sems["f1"], step, True)
            att_vector(dve, step, *combine_vector(dve, sems["f1"], base))
            moe_vector(dve, sems["f2"], step, False)
            next_index, combine = combine_vector(dve, sems["f2"], base)
            for b in range(BATCH):
                next_index(b)
                combine(b)


_INS = ['L0_attn_x', 'L0_attn_Wq', 'L0_attn_Wk', 'L0_attn_Wv', 'L0_attn_Wo', 'L0_attn_lq1', 'L0_attn_lk1',
        'L0_attn_lq2', 'L0_attn_lk2', 'L0_ffn_Wr', 'L0_ffn_br', 'L0_ffn_W1', 'L0_ffn_b1', 'L0_ffn_g1',
        'L0_ffn_be1', 'L0_ffn_W2', 'L0_ffn_b2', 'L0_ffn_g2', 'L0_ffn_be2']
STAGES = ("f1", "at", "f2")


def kernel(**inputs):
    import numpy as _np
    import concourse.bacc as _bacc
    from concourse import mybir as _mybir
    from concourse.bass_utils import run_bass_kernel_spmd as _run

    nc = _bacc.Bacc("TRN2", target_bir_lowering=False, num_devices=1)
    arrays, args = {}, []
    for name in _INS:
        a = _np.ascontiguousarray(inputs[name])
        arrays[f"in_{name}_dram"] = a
        args.append(nc.dram_tensor(f"in_{name}_dram", a.shape, _mybir.dt.from_np(a.dtype), kind="ExternalInput").ap())
    args.append(nc.dram_tensor("out_0_dram", (BATCH, SEQ, DIM), F32, kind="ExternalOutput").ap())
    build(nc, *args, stages=STAGES)
    r = _run(nc, [arrays], core_ids=[0])
    return r.results[0]["out_0_dram"]
```

```python
from contextlib import ExitStack
import math

import concourse.bass as bass
from concourse import mybir

F32 = mybir.dt.float32
BF16 = mybir.dt.bfloat16
I32 = mybir.dt.int32
U32 = mybir.dt.uint32
ALU = mybir.AluOpType
ACT = mybir.ActivationFunctionType
X = mybir.AxisListType.X

P = 128
BATCH, SEQ, DIM = 8, 256, 128
TOK = BATCH * SEQ
TT = TOK // P
NE, TOPK, FF = 8, 2, 512
FC = FF // P
SLOT_TILES = TOPK * TOK // P + NE - 1
EPS = 1e-5
BIG = 3.0e38


HEADS, HD, SUB = 8, 8, 16
VD = DIM // HEADS
SLOTS, MAXSLOT = 8, 6
LAMBDA_INIT = 0.8 - 0.6 * math.exp(-0.3 * 6)
GUARD = 2.0 ** 60
A_STEPS, B_STEPS, D_STEPS = 10, 5, 5


PACK = 8


def experts(eng, eid, n, count):
    v = eng.value_load(eid[0:1, bass.ds(n, 1)], min_val=0, max_val=NE ** PACK - 1)
    return [(v >> (3 * k)) & (NE - 1) for k in range(count)]


class Steps:

    def __init__(self, eng, sem):
        self.eng, self.sem, self.n = eng, sem, 0

    def __call__(self, ins):
        ins.then_inc(self.sem, 1)
        self.n += 1
        self.eng.wait_ge(self.sem, self.n)


class LoopSteps:

    def __init__(self, eng, sem):
        self.eng, self.sem, self.base, self.n = eng, sem, 0, 0

    def start(self, base):
        self.base, self.n = base, 0

    def __call__(self, ins):
        ins.then_inc(self.sem, 1)
        self.n += 1
        self.eng.wait_ge(self.sem, self.base + self.n)


def build(nc, x, Wq, Wk, Wv, Wo, lq1, lk1, lq2, lk2, Wr, br, W1, b1, g1, be1, W2, b2, g2, be2, out, stages=("f1", "at", "f2")):
    with ExitStack() as ctx:
        def sb(name, shape, dt=F32):
            return ctx.enter_context(nc.sbuf_tensor(name, shape, dt))

        def sem(name):
            return ctx.enter_context(nc.semaphore(name))

        bank = [ctx.enter_context(nc.psum_tensor(f"bank{i}", [P, 512], F32)) for i in range(3)]
        quad = ctx.enter_context(nc.psum_tensor("quad", [P, 4, 512], F32))
        bank += [quad[:, i, :] for i in range(4)]
        bank.append(ctx.enter_context(nc.psum_tensor("bank7", [P, 512], F32)))

        xn_dram = nc.dram_tensor("xn_scratch", [TOK, DIM], F32).ap()
        y_dram = nc.dram_tensor("y_scratch", [1 + TOPK * TOK + 40 * P, DIM], F32).ap()

        xs = sb("xs", [P, TT, DIM])
        xn = sb("xn", [P, TT, DIM])
        w1s = sb("w1s", [P, NE * FF])
        w2s = sb("w2s", [P, NE, FC, DIM])
        w2c = sb("w2c", [P, NE * FC * DIM])
        wrs = sb("wrs", [P, NE])
        rows = sb("rows", [96, P])
        cols = sb("cols", [P, 96])
        b2row = sb("b2row", [1, NE * DIM])
        b2p = sb("b2p", [P, NE * DIM])
        g2b = sb("g2b", [P, NE * DIM])
        be2b = sb("be2b", [P, NE * DIM])
        brb = sb("brb", [P, NE])
        b1lo = sb("b1lo", [32, P])
        b1hi = sb("b1hi", [32, 3, P], BF16)
        b1p = sb("b1p", [3, NE * FF], BF16)

        ident = sb("ident", [P, P])
        ones = sb("ones", [P, P])
        mean_w = sb("mean_w", [P, P])
        ones16 = sb("ones16", [P, P], BF16)
        before = sb("before", [P, P], BF16)
        eps_c = sb("eps_c", [P, 1])
        e_lt = sb("e_lt", [P, NE, NE])
        first_w = sb("first_w", [P, NE])
        lo_iota = sb("lo_iota", [P, P])
        tile_iota = sb("tile_iota", [P, 48])
        row_id = sb("row_id", [P, 1])
        spare = sb("spare", [P, 40])

        xnT = sb("xnT", [P, 4, P])
        stats = sb("stats", [P, TT, 6])
        mv = sb("mv", [P, TT, 2])
        sdev = sb("sdev", [P, TT])
        rstd = sb("rstd", [P, TT])
        lg = sb("lg", [P, TT, NE])
        lg2 = sb("lg2", [P, TT, NE])
        eq = sb("eq", [P, TT, NE])
        oh = sb("oh", [P, TOPK, TT, NE])
        m12 = sb("m12", [P, TOPK, TT])
        mw = sb("mw", [P, TT])
        picked = sb("picked", [P, TT, NE], BF16)
        gate = sb("gate", [P, TOPK, TT])
        gden = sb("gden", [P, TT])
        ntile = sb("ntile", [P, NE])
        ntile_i = sb("ntile_i", [P, NE], I32)
        start = sb("start", [P, NE])
        end = sb("end", [P, NE])
        tri = sb("tri", [P, NE, NE])
        rank = sb("rank", [P, TT, NE])
        posf = sb("posf", [P, TOPK * TT])
        posi = sb("posi", [P, TOPK * TT], I32)
        hi_i = sb("hi_i", [P, TOPK * TT], I32)
        hi_f = sb("hi_f", [P, TOPK * TT])
        lo_f = sb("lo_f", [P, TOPK * TT])
        oh_lo = sb("oh_lo", [P, TOPK * TT, P], BF16)
        oh_hi = sb("oh_hi", [P, TOPK * TT, 2, 40], BF16)
        tcol = sb("tcol", [P, TOPK * TT])
        slot_t = sb("slot_t", [P, 40])
        slot_f = sb("slot_f", [P, 40])
        slot_i = sb("slot_i", [P, 40], U32)
        slot_u = sb("slot_u", [P, 40], U32)
        dest_f = sb("dest_f", [P, 40])
        dest_u = sb("dest_u", [P, 40], U32)
        ecmp = sb("ecmp", [1, 48, NE])
        eidf = sb("eidf", [1, 48])
        epk = sb("epk", [1, 2, 40])
        eid = sb("eid", [1, 40], I32)

        xg = sb("xg", [P, 4, DIM])
        xT = sb("xT", [P, 2, P])
        hh = sb("hh", [P, 2, FF])
        hT = sb("hT", [P, 2, FF])
        st1 = sb("st1", [P, 2, 6])
        mv1 = sb("mv1", [P, 2, 2])
        sd1 = sb("sd1", [P, 2, 1])
        r1 = sb("r1", [P, 2, 1])
        yy = sb("yy", [P, 2, DIM])
        st2 = sb("st2", [P, 2, 6])
        mv2 = sb("mv2", [P, 2, 2])
        sd2 = sb("sd2", [P, 2, 1])
        r2 = sb("r2", [P, 2, 1])
        yz = sb("yz", [P, 2, DIM])
        yo = sb("yo", [P, 2, DIM])
        yk = sb("yk", [P, TOPK, TT, DIM])
        ysum = sb("ysum", [P, 2, DIM])

        s_ld_x = sem("s_ld_x")
        s_ld_w = sem("s_ld_w")
        s_ld_w2 = sem("s_ld_w2")
        s_ld_w1 = sem("s_ld_w1")
        s_bc = sem("s_bc")
        s_ld_a = sem("s_ld_a")
        s_lam = sem("s_lam")
        s_const = sem("s_const")
        s_pool = sem("s_pool")
        s_dve = sem("s_dve")
        s_cols = sem("s_cols")
        s_colc = sem("s_colc")
        s_b1 = sem("s_b1")
        s_b1d = sem("s_b1d")
        s_w2g = sem("s_w2g")
        s_mean = sem("s_mean")
        s_w2c = sem("s_w2c")
        s_b2m = sem("s_b2m")
        s_b2c = sem("s_b2c")
        s_out = sem("s_out")

        ident16 = sb("ident16", [P, P], BF16)
        mask_q = sb("mask_q", [P, P], BF16)
        mask_k = sb("mask_k", [P, P], BF16)
        neg_half = sb("neg_half", [P, 32])
        wrow = sb("wrow", [P, 4, DIM])
        wqkvo = sb("wqkvo", [P, 4, DIM])
        lam_in = sb("lam_in", [P, 4, HD])
        lam_p = sb("lam_p", [P, 2, HD])
        lam_s = sb("lam_s", [P, 2])
        lam_e = sb("lam_e", [P, 2])
        neg_lam = sb("neg_lam", [P, 1])
        ast = sb("ast", [P, 2, 6])
        amv = sb("amv", [P, 2, 2])
        ave = sb("ave", [P, 2])
        ars = sb("ars", [P, 2])
        axn = sb("axn", [P, 2, DIM])
        axT = sb("axT", [P, 2 * P])
        qk = sb("qk", [P, 2, 2, DIM])
        part = sb("part", [P, 3, 2, 2 * DIM], BF16)
        q6 = sb("q6", [P, 2 * SUB, SLOTS, HD], BF16)
        k6 = sb("k6", [P, 2 * SUB, SLOTS, HD], BF16)
        vaug = sb("vaug", [P, 2, 2, HEADS, 32])
        oTs = sb("oTs", [P, 2, 2, 2 * P])
        kT = sb("kT", [P, 2, HEADS, 2 * P], BF16)
        qT = sb("qT", [P, 2, HEADS, 2 * P], BF16)
        mxT = sb("mxT", [P, 3 * P], BF16)
        sel = sb("sel", [P, HEADS], BF16)
        sel2 = sb("sel2", [P, 2, HEADS])
        mx = sb("mx", [P, 2 * SUB])
        mpart = sb("mpart", [P, 2, P], BF16)
        prob = sb("prob", [P, 2, 2, 3 * P])
        rsum = sb("rsum", [P, 2, SUB])
        ow = sb("ow", [P, 2, SUB, VD])
        od = sb("od", [P, 2, HEADS, VD])
        osq = sb("osq", [P, 2, HEADS, VD])
        oms = sb("oms", [P, 2 * HEADS])
        orr = sb("orr", [P, 2 * HEADS])
        vnew = sb("vnew", [P, 2, DIM])
        oT = sb("oT", [P, 2 * P])
        a_names = ("wT wTc lam lame var rs xn xTp xTc proj qkv vc kcopy kTp kTc qTp qTc s smax mparts mTp mTc "
                   "st prob o oTv ot ow msq rms onorm oTp oTc res x2 vaug astep bstep dstep").split()
        A = {n: sem(f"at_{n}") for n in a_names}

        names = ("mv sd xn xnst xnTp xnTc lgp top gexp gate picked rankp oh slotp slot eid "
                 "xg0 xg1 xg2 xg3 xTp xTc h relu bn mv1 sq1 hTp hTc A ya mv2 sq2 yz yf yst0 yst1 "
                 "dest yld0 yld1 pcomb comb lstep").split()
        sems = {k: {n: sem(f"{k}_{n}") for n in names} for k in stages if k != "at"}
        block = ctx.enter_context(nc.Block())

        NCONST = 17

        def moe_sync(sp, S, last):
            sp.wait_ge(S["xn"], TT)
            sp.dma_start(xn_dram.rearrange("(t p) d -> p t d", p=P), xn[:]).then_inc(S["xnst"], 16)
            sp.wait_ge(S["yst0"], 16 * ((SLOT_TILES + 1) // 2))
            sp.wait_ge(S["yst1"], 16 * (SLOT_TILES // 2))
            rows_k = y_dram[1:1 + TOPK * TOK, :].rearrange("(k t p) d -> p k t d", k=TOPK, p=P)
            for b in range(BATCH):
                if b >= 2:
                    sp.wait_ge(S[f"yld{b % 2}"], b // 2 * 32)
                for k in range(TOPK):
                    sp.dma_start(yk[:, k, 2 * b:2 * b + 2, :], rows_k[:, k, 2 * b:2 * b + 2, :]).then_inc(S[f"yld{b % 2}"], 16)
            if last:
                for b in range(BATCH):
                    sp.wait_ge(S["comb"], 2 * b + 2)
                    sp.dma_start(out[b].rearrange("(u p) d -> p u d", p=P), xs[:, 2 * b:2 * b + 2, :]).then_inc(s_out, 16)

        def moe_gpsimd(pool, S):
            pool.wait_ge(S["xnst"], 16)
            pool.wait_ge(S["slot"], 1)

            def gather(n, u):
                pool.indirect_dma_start(out=xg[:, u, :], out_offset=None, in_=xn_dram,
                                        in_offset=bass.IndirectOffsetOnAxis(ap=slot_u[:, n:n + 1], axis=0)
                                        ).then_inc(S[f"xg{u}"], 16)

            def store(n, u):
                pool.wait_ge(S["yf"], n + 1)
                pool.indirect_dma_start(out=y_dram, out_offset=bass.IndirectOffsetOnAxis(ap=dest_u[:, n:n + 1], axis=0),
                                        in_=yo[:, u, :], in_offset=None).then_inc(S[f"yst{u}"], 16)

            for n in range(4):
                gather(n, n)
            pool.wait_ge(S["dest"], 1)
            for n in range(SLOT_TILES):
                if n + 4 < SLOT_TILES:
                    pool.wait_ge(S["xTp"], n + 1)
                    gather(n + 4, n % 4)
                if n >= 2:
                    store(n - 2, n % 2)
            store(SLOT_TILES - 2, 1)
            store(SLOT_TILES - 1, 0)

        def moe_scalar(act, S):
            act.wait_ge(S["mv"], TT)
            act.activation(sdev[:], mv[:, :, 1], ACT.Sqrt, bias=eps_c[:]).then_inc(S["sd"], 1)
            for g in range(4):
                act.wait_ge(S["xnTp"], g + 1)
                if g:
                    act.wait_ge(S["lgp"], g)
                act.copy(xnT[:], bank[g % 2][:].rearrange("p (a b) -> p a b", a=4)).then_inc(S["xnTc"], 1)
            act.wait_ge(S["top"], 1)
            act.activation(gden[:], mw[:], ACT.Exp).then_inc(S["gexp"], 1)

            def copy_xT(m, u):
                act.wait_ge(S["xTp"], m + 1)
                if not (isinstance(m, int) and m < 2):
                    act.wait_ge(S["h"], m - 1)
                act.copy(xT[:, u, :], bank[0][:, 0:P]).then_inc(S["xTc"], 1)

            def relu(m, u):
                act.wait_ge(S["h"], m + 1)
                if not (isinstance(m, int) and m < 2):
                    act.wait_ge(S["hTp"], m - 1)
                    act.wait_ge(S["bn"], m - 1)
                act.activation(hh[:, u, :], bank[1 + u][:], ACT.Relu).then_inc(S["relu"], 1)

            def sqrt1(m, u):
                act.wait_ge(S["mv1"], m + 1)
                act.activation(sd1[:, u, :], mv1[:, u, 1:2], ACT.Sqrt, bias=eps_c[:]).then_inc(S["sq1"], 1)

            def sqrt2(m, u):
                act.wait_ge(S["mv2"], m + 1)
                act.activation(sd2[:, u, :], mv2[:, u, 1:2], ACT.Sqrt, bias=eps_c[:]).then_inc(S["sq2"], 1)

            def body(n, u, do_x=True, do_h=True, lag=True):
                act.wait_ge(S["hTp"], n + 1)
                if not (isinstance(n, int) and n < 2):
                    act.wait_ge(S["A"], n - 1)
                act.copy(hT[:, u, :], bank[3 + u][:]).then_inc(S["hTc"], 1)
                if do_x:
                    copy_xT(n + 2, u)
                sqrt1(n, u)
                if do_h:
                    relu(n + 1, 1 - u)
                if lag:
                    sqrt2(n - 1, 1 - u)

            copy_xT(0, 0)
            copy_xT(1, 1)
            relu(0, 0)
            body(0, 0, lag=False)
            body(1, 1)
            with act.Fori(1, (SLOT_TILES - 3) // 2) as i:
                for u in range(2):
                    body(i * 2 + u, u)
            for n in range(SLOT_TILES - 3, SLOT_TILES):
                body(n, n % 2, do_x=n + 2 < SLOT_TILES, do_h=n + 1 < SLOT_TILES)
            sqrt2(SLOT_TILES - 1, (SLOT_TILES - 1) % 2)

        def moe_tensor(pe, S, first):
            pe.wait_ge(s_const, NCONST)
            for g in range(4):
                pe.wait_ge(S["xn"], 4 * g + 4)
                if g >= 2:
                    pe.wait_ge(S["xnTc"], g - 1)
                for j in range(4):
                    last = pe.transpose(bank[g % 2][:, j * P:(j + 1) * P], xn[:, 4 * g + j, :], ident[:])
                last.then_inc(S["xnTp"], 1)
                pe.wait_ge(S["xnTc"], g + 1)
                for j in range(4):
                    t = 4 * g + j
                    last = pe.matmul(bank[2][:, t * NE:(t + 1) * NE], xnT[:, j, :], wrs[:], start=True, stop=True)
                last.then_inc(S["lgp"], 1)
            pe.wait_ge(S["picked"], 1)
            pe.matmul(bank[3][:, 0:NE], before[:], picked[:, 0, :], start=True, stop=True)
            pe.matmul(bank[3][:, NE:TT * NE], before[:], picked[:, 1:TT, :], start=True, stop=False)
            for t in range(TT - 2, -1, -1):
                w = TT - 1 - t
                pe.matmul(bank[3][:, (t + 1) * NE:TT * NE].rearrange("p (a b) -> p a b", b=NE), ones16[:],
                          picked[:, t:t + 1, :].to_broadcast([P, w, NE]), start=False, stop=(t == 0),
                          skip_group_check=(t > 0))
            for t in range(TT):
                last = pe.matmul(bank[4][:, 0:NE], ones16[:], picked[:, t, :], start=(t == 0), stop=(t == TT - 1))
            last.then_inc(S["rankp"], 1)
            for c in range(TOPK * TT):
                if c % 8 == 0:
                    pe.wait_ge(S["oh"], c // 8 + 1)
                last = pe.matmul(bank[5][:, 0:80], oh_lo[:, c, :], oh_hi[:, c, :, :], start=(c == 0), stop=(c == TOPK * TT - 1))
            last.then_inc(S["slotp"], 1)
            pe.wait_ge(S["eid"], 1)
            if first:
                weights_tensor(pe)
                pe.wait_ge(s_ld_w1, 16)
            pe.wait_ge(s_w2c, 2)
            pe.wait_ge(s_b1d, 48)
            pe.wait_ge(s_b2c, 1)

            def turn_x(m, i, q):
                pe.wait_ge(S[f"xg{q}"], i * 16 + 16)
                if not (isinstance(m, int) and m == 0):
                    pe.wait_ge(S["xTc"], m)
                pe.transpose(bank[0][:, 0:P], xg[:, q, :], ident[:]).then_inc(S["xTp"], 1)

            def hidden(m, u, e):
                pe.wait_ge(S["xTc"], m + 1)
                if not (isinstance(m, int) and m < 2):
                    pe.wait_ge(S["relu"], m - 1)
                pe.matmul(bank[1 + u][:], ones16[0:3, :], b1p[:, bass.ds(e * FF, FF)], start=True, stop=False)
                pe.matmul(bank[1 + u][:], xT[:, u, :], w1s[:, bass.ds(e * FF, FF)], start=False, stop=True).then_inc(S["h"], 1)

            def turn_h(n, u):
                pe.wait_ge(S["relu"], n + 1)
                if not (isinstance(n, int) and n == 0):
                    pe.wait_ge(S["hTc"], n)
                for c in range(FC):
                    last = pe.transpose(bank[3 + u][:, c * P:c * P + P], hh[:, u, c * P:(c + 1) * P], ident[:])
                last.then_inc(S["hTp"], 1)

            def second(n, u, e):
                pe.wait_ge(S["hTc"], n + 1)
                if not (isinstance(n, int) and n < 2):
                    pe.wait_ge(S["ya"], n - 1)
                for c in range(FC):
                    last = pe.matmul(bank[5 + u][:, 0:DIM], hT[:, u, c * P:(c + 1) * P],
                                     w2c[:, bass.ds(e * (FC * DIM) + c * DIM, DIM)], start=(c == 0), stop=(c == FC - 1))
                last.then_inc(S["A"], 1)

            def body(n, i, q, e, do_x=True, do_h=True):
                turn_h(n, q % 2)
                if do_x:
                    turn_x(n + 2, i + (q + 2) // 4, (q + 2) % 4)
                if do_h:
                    hidden(n + 1, 1 - q % 2, e[1])
                second(n, q % 2, e[0])

            turn_x(0, 0, 0)
            turn_x(1, 0, 1)
            e = experts(pe, eid, 0, 5)
            hidden(0, 0, e[0])
            for n in range(4):
                body(n, 0, n, e[n:])
            with pe.Fori(1, (SLOT_TILES - 3) // 4) as i:
                e = experts(pe, eid, i * 4, 5)
                for q in range(4):
                    body(i * 4 + q, i, q, e[q:])
            e = experts(pe, eid, SLOT_TILES - 3, 3)
            for n in range(SLOT_TILES - 3, SLOT_TILES):
                body(n, n // 4, n % 4, e[n - SLOT_TILES + 3:], do_x=n + 2 < SLOT_TILES, do_h=n + 1 < SLOT_TILES)

        def moe_vector(dve, S, step, first):
            if first:
                dve.wait_ge(s_ld_x, 16)
            for t in range(TT):
                dve.bn_stats(stats[:, t, :], xs[:, t, :]).then_inc(S["lstep"], 1)
            for t in range(TT):
                dve.wait_ge(S["lstep"], t + 1)
                dve.bn_aggr(mv[:, t, :], stats[:, t, :]).then_inc(S["mv"], 1)
            dve.wait_ge(S["sd"], 1)
            step(dve.reciprocal(rstd[:], sdev[:]))
            for t in range(TT):
                dve.tensor_scalar(xn[:, t, :], xs[:, t, :], mv[:, t, 0:1], rstd[:, t:t + 1],
                                  ALU.subtract, ALU.mult).then_inc(S["xn"], 1)
            dve.wait_ge(S["lgp"], 4)
            dve.wait_ge(s_const, NCONST)
            step(dve.tensor_tensor(lg[:], bank[2][:, 0:TT * NE].rearrange("p (a b) -> p a b", b=NE),
                                   brb[:, None, :].to_broadcast([P, TT, NE]), ALU.add))
            for k in range(TOPK):
                src = lg if k == 0 else lg2
                step(dve.tensor_reduce(m12[:, k, :], src[:], X, ALU.max))
                step(dve.tensor_tensor(eq[:], src[:], m12[:, k, :, None].to_broadcast([P, TT, NE]), ALU.is_equal))
                step(dve.tensor_tensor(eq[:], eq[:], first_w[:, None, :].to_broadcast([P, TT, NE]), ALU.mult))
                step(dve.tensor_reduce(mw[:], eq[:], X, ALU.max))
                step(dve.tensor_tensor(oh[:, k], eq[:], mw[:, :, None].to_broadcast([P, TT, NE]), ALU.is_equal))
                if k == 0:
                    step(dve.scalar_tensor_tensor(lg2[:], oh[:, 0], -BIG, lg[:], ALU.mult, ALU.add))
            dve.tensor_tensor(picked[:], oh[:, 0], oh[:, 1], ALU.add).then_inc(S["picked"], 1)
            dve.tensor_tensor(mw[:], m12[:, 1, :], m12[:, 0, :], ALU.subtract).then_inc(S["top"], 1)
            dve.wait_ge(S["rankp"], 1)
            step(dve.tensor_scalar(ntile_i[:], bank[4][:, 0:NE], float(P - 1), None, ALU.add))
            step(dve.tensor_scalar(ntile_i[:], ntile_i[:], 7, None, ALU.arith_shift_right))
            step(dve.tensor_copy(ntile[:], ntile_i[:]))
            step(dve.tensor_tensor(tri[:], e_lt[:], ntile[:, None, :].to_broadcast([P, NE, NE]), ALU.mult))
            step(dve.tensor_reduce(start[:], tri[:], X, ALU.add))
            step(dve.tensor_tensor(end[:], start[:], ntile[:], ALU.add))
            step(dve.scalar_tensor_tensor(rank[:], start[:, None, :].to_broadcast([P, TT, NE]), float(P),
                                          bank[3][:, 0:TT * NE].rearrange("p (a b) -> p a b", b=NE), ALU.mult, ALU.add))
            for k in range(TOPK):
                step(dve.tensor_tensor(eq[:], oh[:, k], rank[:], ALU.mult))
                step(dve.tensor_reduce(posf[:, k * TT:(k + 1) * TT], eq[:], X, ALU.add))
            step(dve.tensor_copy(posi[:], posf[:]))
            step(dve.tensor_scalar(hi_i[:], posi[:], 7, None, ALU.arith_shift_right))
            step(dve.tensor_copy(hi_f[:], hi_i[:]))
            step(dve.scalar_tensor_tensor(lo_f[:], hi_f[:], -float(P), posf[:], ALU.mult, ALU.add))
            for q in range(4):
                c = slice(8 * q, 8 * q + 8)
                step(dve.tensor_tensor(oh_lo[:, c, :], lo_f[:, c, None].to_broadcast([P, 8, P]),
                                       lo_iota[:, None, :].to_broadcast([P, 8, P]), ALU.is_equal))
                step(dve.tensor_tensor(oh_hi[:, c, 1, :], hi_f[:, c, None].to_broadcast([P, 8, 40]),
                                       tile_iota[:, None, 0:40].to_broadcast([P, 8, 40]), ALU.is_equal))
                step(dve.tensor_tensor(oh_hi[:, c, 0, :], oh_hi[:, c, 1, :],
                                       tcol[:, c, None].to_broadcast([P, 8, 40]), ALU.mult))
                dve.tensor_scalar(oh_hi[:, c, 1, :], oh_hi[:, c, 1, :], row_id[:], None, ALU.mult).then_inc(S["oh"], 1)
            step(dve.tensor_tensor(ecmp[:], tile_iota[0:1, :, None].to_broadcast([1, 48, NE]),
                                   end[0:1, None, :].to_broadcast([1, 48, NE]), ALU.is_ge))
            step(dve.tensor_reduce(eidf[:], ecmp[:], X, ALU.add))
            step(dve.tensor_scalar(eidf[:], eidf[:], float(NE - 1), None, ALU.min))
            src = eidf[:, PACK - 1:PACK + 39]
            for j in range(PACK - 2, -1, -1):
                dst = eid if j == 0 else epk[:, j % 2]
                ins = dve.scalar_tensor_tensor(dst[:], src, float(NE), eidf[:, j:j + 40], ALU.mult, ALU.add)
                if j:
                    step(ins)
                src = dst
            ins.then_inc(S["eid"], 1)
            dve.wait_ge(S["slotp"], 1)
            step(dve.tensor_copy(slot_t[:], bank[5][:, 40:80]))
            step(dve.scalar_tensor_tensor(slot_f[:], bank[5][:, 0:40], float(P), slot_t[:], ALU.mult, ALU.add))
            step(dve.tensor_scalar(slot_i[:], slot_f[:], float(TOK - 1), None, ALU.add))
            dve.tensor_scalar(slot_u[:], slot_i[:], TOK - 1, None, ALU.bitwise_and).then_inc(S["slot"], 1)
            step(dve.scalar_tensor_tensor(dest_f[:], slot_f[:], 0.0, spare[:], ALU.is_equal, ALU.mult))
            dve.tensor_tensor(dest_u[:], dest_f[:], slot_f[:], ALU.add).then_inc(S["dest"], 1)
            dve.wait_ge(S["gexp"], 1)
            step(dve.tensor_scalar(m12[:, 0, :], gden[:], 2.0, 2.0, ALU.mult, ALU.add))
            step(dve.reciprocal(gate[:, 0, :], m12[:, 0, :]))
            dve.tensor_tensor(gate[:, 1, :], gate[:, 0, :], gden[:], ALU.mult).then_inc(S["gate"], 1)
            if first:
                weights_vector(dve, step)

            ls = LoopSteps(dve, S["lstep"])
            PER = 4

            def stats1(m, u):
                dve.wait_ge(S["relu"], m + 1)
                if not (isinstance(m, int) and m < 2):
                    dve.wait_ge(S["sq1"], m - 1)
                dve.bn_stats(st1[:, u, :], hh[:, u, :]).then_inc(S["bn"], 1)
                dve.wait_ge(S["bn"], m + 1)
                dve.memset(hold[:, 0:1], 0.0)
                dve.bn_aggr(mv1[:, u, :], st1[:, u, :]).then_inc(S["mv1"], 1)

            def y_part(m, u, e):
                ls.start(m * PER + TT)
                dve.wait_ge(S["sq1"], m + 1)
                ls(dve.reciprocal(r1[:, u, :], sd1[:, u, :]))
                dve.wait_ge(S["A"], m + 1)
                dve.scalar_tensor_tensor(yy[:, u, :], bank[5 + u][:, 0:DIM], r1[:, u, :],
                                         b2p[:, bass.ds(e * DIM, DIM)], ALU.mult, ALU.add).then_inc(S["ya"], 1)
                dve.wait_ge(S["ya"], m + 1)
                ls(dve.tensor_scalar(yy[:, u, :], yy[:, u, :], 0.0, None, ALU.max))
                dve.bn_stats(st2[:, u, :], yy[:, u, :]).then_inc(S["lstep"], 1)
                dve.wait_ge(S["lstep"], m * PER + TT + 3)
                dve.memset(hold[:, 1:2], 0.0)
                dve.bn_aggr(mv2[:, u, :], st2[:, u, :]).then_inc(S["mv2"], 1)

            def y_norm(m, u, e):
                ls.base, ls.n = m * PER + TT, 3
                dve.wait_ge(S["mv2"], m + 1)
                dve.scalar_tensor_tensor(yz[:, u, :], yy[:, u, :], mv2[:, u, 0:1], g2b[:, bass.ds(e * DIM, DIM)],
                                         ALU.subtract, ALU.mult).then_inc(S["yz"], 1)
                dve.wait_ge(S["sq2"], m + 1)
                ls(dve.reciprocal(r2[:, u, :], sd2[:, u, :]))
                if not (isinstance(m, int) and m < 2):
                    dve.wait_ge(S[f"yst{u}"], (m - u) * 8)
                dve.scalar_tensor_tensor(yo[:, u, :], yz[:, u, :], r2[:, u, :], be2b[:, bass.ds(e * DIM, DIM)],
                                         ALU.mult, ALU.add).then_inc(S["yf"], 1)

            def body(n, u, e=None, do_h=True):
                if e is not None:
                    y_part(n - 1, 1 - u, e)
                if do_h:
                    stats1(n + 1, 1 - u)
                if e is not None:
                    y_norm(n - 1, 1 - u, e)

            stats1(0, 0)
            e = experts(dve, eid, 0, 3)
            body(0, 0)
            for n in range(1, 4):
                body(n, n % 2, e[n - 1])
            with dve.Fori(1, (SLOT_TILES - 3) // 4) as i:
                e = experts(dve, eid, i * 4 - 1, 4)
                for q in range(4):
                    body(i * 4 + q, q % 2, e[q])
            e = experts(dve, eid, SLOT_TILES - 4, 4)
            for n in range(SLOT_TILES - 3, SLOT_TILES):
                body(n, n % 2, e[n - SLOT_TILES + 3], do_h=n + 1 < SLOT_TILES)
            y_part(SLOT_TILES - 1, 0, e[3])
            y_norm(SLOT_TILES - 1, 0, e[3])

        def combine_vector(dve, S, b):
            dve.wait_ge(S[f"yld{b % 2}"], 32 * (b // 2) + 32)
            for k in range(TOPK):
                for t in (2 * b, 2 * b + 1):
                    if k:
                        dve.wait_ge(S["pcomb"], t + 1)
                    dve.scalar_tensor_tensor(xs[:, t, :], yk[:, k, t, :], gate[:, k, t:t + 1], xs[:, t, :], ALU.mult, ALU.add
                                             ).then_inc(S["comb" if k else "pcomb"], 1)

        def turns(eng, turn):
            for t in range(3):
                turn(t, t % 2)
            with eng.Fori(0, (BATCH - 3) // 2) as i:
                for u in range(2):
                    turn(i * 2 + (3 + u), (3 + u) % 2)
            for t in range(BATCH - 1, BATCH + 3):
                turn(t, t % 2)

        def stages_of(t):
            return [not isinstance(t, int) or 0 <= t - k < BATCH for k in range(4)]

        def att_gpsimd(pool, S):
            def combine(b, par):
                hold_pool(S[f"yld{par}"], (b - par) * 16 + 32)
                y = yk[:, :, bass.ds(b * 2, 2), :]
                pool.tensor_tensor(y, y, gate[:, :, bass.ds(b * 2, 2)][:, :, :, None].to_broadcast([P, TOPK, 2, DIM]), ALU.mult).then_inc(S["pcomb"], 1)
                hold_pool(S["pcomb"], b * 2 + 1)
                pool.tensor_tensor(ysum[:], y[:, 0], y[:, 1], ALU.add).then_inc(S["pcomb"], 1)
                hold_pool(S["pcomb"], b * 2 + 2)
                x2 = xs[:, bass.ds(b * 2, 2), :]
                pool.tensor_tensor(x2, x2, ysum[:], ALU.add).then_inc(S["comb"], 1)

            def hold_pool(semaphore, n):
                pool.wait_ge(semaphore, n)
                pool.tensor_tensor(gpad[:, 1:2], eps_c[0:1, :], eps_c[0:1, :], ALU.add)

            def turn(t, par):
                A_, B_, C_, D_ = stages_of(t)
                if A_:
                    pool.wait_ge(A["var"], t + 1)
                    pool.tensor_tensor(ars[:], ave[:], neg_half[:, 0:2], ALU.pow).then_inc(A["rs"], 1)
                if D_:
                    pool.wait_ge(A["msq"], t - 2)
                    pool.tensor_tensor(orr[:], oms[:], neg_half[:, 0:2 * HEADS], ALU.pow).then_inc(A["rms"], 1)
                if A_ and not (isinstance(t, int) and t == BATCH - 1):
                    combine(t + 1, 1 - par)
            combine(0, 0)
            turns(pool, turn)

        def att_scalar(act):
            act.wait_ge(A["wT"], 1)
            for j, scale in ((0, HD ** -0.5), (3, 1.0 - LAMBDA_INIT)):
                act.activation(wqkvo[:, j], bank[7][:, j * P:(j + 1) * P], ACT.Copy, scale=scale)
            act.copy(wqkvo[:, 1:3], bank[7][:, P:3 * P].rearrange("p (a b) -> p a b", a=2)).then_inc(A["wTc"], 1)
            act.wait_ge(A["lam"], 1)
            act.activation(lam_e[:], lam_s[:], ACT.Exp).then_inc(A["lame"], 1)

            def turn(t, par):
                A_, B_, C_, D_ = stages_of(t)
                b, c, d = t - 1, t - 2, t - 3

                def turned(dst, src, name, u, seq, slot):
                    act.wait_ge(A[name + "Tp"], seq * 2 + u + 1)
                    act.copy(dst[:, slot, :, u * P:u * P + P], src.bitcast(BF16).rearrange("p (a e) -> p a e", e=P)
                             ).then_inc(A[name + "Tc"], 1)

                def expo(g):
                    act.wait_ge(A["st"], c * 8 + g + 1)
                    if g >= 2 or not (isinstance(c, int) and c == 0):
                        act.wait_ge(A["o"], c * 8 + g - 1)
                    act.activation(prob[:, g % 2], quad[:, 0:2, 0:3 * P], ACT.Exp).then_inc(A["prob"], 1)

                def half_values(s, seq):
                    act.wait_ge(A["o"], seq * 8 + 4 * s + 4)
                    act.copy(oTs[:, s].rearrange("p a e -> p (a e)"), bank[7 if s == 0 else 0][:]).then_inc(A["oTv"], 1)

                if D_:
                    half_values(1, d)
                if B_:
                    turned(qT, bank[5][:], "q", 0, b, 1 - par)
                if C_:
                    act.wait_ge(A["mTp"], c + 1)
                    act.copy(mxT[:], bank[1][:, 0:3 * P // 2].bitcast(BF16)).then_inc(A["mTc"], 1)
                if B_:
                    turned(kT, bank[6][:], "k", 1, b, 1 - par)
                if C_:
                    expo(0)
                    expo(1)
                if B_:
                    turned(qT, bank[2][:], "q", 1, b, 1 - par)
                if A_:
                    act.wait_ge(A["xTp"], t + 1)
                    act.copy(axT[:], bank[1][:, 0:2 * P]).then_inc(A["xTc"], 1)
                if C_:
                    expo(2)
                    expo(3)
                if A_:
                    for u in range(2):
                        act.wait_ge(A["proj"], t * 2 + u + 1)
                        if u == 0 and B_:
                            act.wait_ge(A["vaug"], t)
                        o = bank[1 + u]
                        act.copy(qk[:, :, u, :], o[:, 0:2 * DIM].rearrange("p (a b) -> p a b", a=2)).then_inc(A["qkv"], 1)
                        act.copy(vnew[:, u, :], o[:, 2 * DIM:3 * DIM]).then_inc(A["vc"], 1)
                if C_:
                    expo(4)
                    half_values(0, c)
                    expo(5)
                if D_:
                    act.wait_ge(A["oTp"], d + 1)
                    act.copy(oT[:], bank[1][:, 0:2 * P]).then_inc(A["oTc"], 1)
                if C_:
                    expo(6)
                    expo(7)
                if A_:
                    turned(kT, bank[2][:], "k", 0, t, par)
            turns(act, turn)

        def att_tensor(pe):
            pe.wait_ge(s_ld_a, 80)
            for j in range(4):
                last = pe.transpose(bank[7][:, j * P:(j + 1) * P], wrow[:, j, :], ident[:])
            last.then_inc(A["wT"], 1)
            pe.wait_ge(A["wTc"], 1)

            def turn8(src, u, dst):
                for hp in range(HEADS):
                    last = pe.transpose(dst.bitcast(BF16)[:, hp * P:hp * P + P],
                                        src[:, u * SUB + 2 * hp:u * SUB + 2 * hp + 2].rearrange("p a s e -> p (a s e)"), ident16[:])
                return last

            def turn(t, par):
                A_, B_, C_, D_ = stages_of(t)
                b, c, d = t - 1, t - 2, t - 3
                kb, qb, kc, qc = kT[:, 1 - par], qT[:, 1 - par], kT[:, par], qT[:, par]

                def scores(n):
                    u, h0, per = (0, 8 * n, 4) if n < 2 else (1, 4 * (n - 2), 2)
                    w = (u + 1) * P
                    if n:
                        pe.wait_ge(A["smax"], b * 6 + n)
                    for a in range(per):
                        hs = [(h, slice(64 * (h % 2), 64 * (h % 2) + MAXSLOT * HD), bank[5 + h % 2][:, a * w:(a + 1) * w])
                              for h in (h0 + 2 * a, h0 + 2 * a + 1)]
                        if u:
                            for h, r, o in hs:
                                pe.matmul(o[:, 0:P], qb[r, h // 2, P:2 * P], kb[r, h // 2, 0:P], start=True, stop=True)
                        for h, r, o in hs:
                            pe.matmul(o[:, w - P:w], ident16[:], mask_q[:], start=True, stop=False)
                        for h, r, o in hs:
                            last = pe.matmul(o[:, w - P:w], qb[r, h // 2, u * P:u * P + P], kb[r, h // 2, u * P:u * P + P],
                                             start=False, stop=True)
                    last.then_inc(A["s"], 1)

                def scores_t(g):
                    if g:
                        pe.wait_ge(A["prob"], c * 8 + g)
                    hs = [(64 * p, bank[3 + p][:, 0:3 * P]) for p in range(2)]
                    for r, o in hs:
                        pe.matmul(o, sel[r:r + 64, g:g + 1].to_broadcast([64, P]), mxT[r:r + 64, :], start=True, stop=False)
                    for r, o in hs:
                        pe.matmul(o.rearrange("p (a e) -> p a e", e=P)[:, 0:3:2, :], ident16[:],
                                  mask_k[:, None, :].to_broadcast([P, 2, P]), start=False, stop=False)
                    for r, o in hs:
                        pe.matmul(o[:, 0:2 * P], kc[r:r + 48, g, 0:P], qc[r:r + 48, g, :], start=False, stop=False)
                    for r, o in hs:
                        last = pe.matmul(o[:, 2 * P:3 * P], kc[r:r + 48, g, P:2 * P], qc[r:r + 48, g, P:2 * P], start=False, stop=True)
                    last.then_inc(A["st"], 1)

                def values(g):
                    pe.wait_ge(A["prob"], c * 8 + g + 1)
                    v0, v1 = (vaug[:, par, u, g, :] for u in range(2))
                    o = bank[7 if g < 4 else 0][32 * (g % 4):32 * (g % 4) + 32, :].rearrange("p (a e) -> p a e", a=2)
                    pr = prob[:, g % 2]
                    at = dict(tile_position=(0, 32 * (g % 4)))
                    pe.matmul(o[:, :, 0:P], v0, pr[:, :, 0:P], start=True, stop=True, **at)
                    pe.matmul(o[:, :, P:2 * P], v0, pr[:, :, P:2 * P], start=True, stop=False, **at)
                    pe.matmul(o[:, :, P:2 * P], v1, pr[:, :, 2 * P:3 * P], start=False, stop=True, **at).then_inc(A["o"], 1)

                if D_:
                    pe.wait_ge(A["oTv"], d * 2 + 2)
                    for u, bk in enumerate((7, 0)):
                        for r in range(4):
                            last = pe.transpose(bank[bk][:, r * P:r * P + P], oTs[:, r // 2, r % 2, u * P:u * P + P], ident[:])
                    last.then_inc(A["ot"], 1)
                if C_:
                    pe.wait_ge(A["mparts"], t - 1)
                    for j, u in enumerate((0, 1, 1)):
                        last = pe.transpose(bank[1][:].bitcast(BF16)[:, j * P:j * P + P], mpart[:, u, :], ident16[:])
                    last.then_inc(A["mTp"], 1)
                if B_:
                    pe.wait_ge(A["kTc"], b * 2 + 1)
                    turn8(q6, 1, bank[2][:]).then_inc(A["qTp"], 1)
                if C_:
                    pe.wait_ge(A["mTc"], t - 1)
                    scores_t(0)
                if B_:
                    pe.wait_ge(A["kTc"], t * 2)
                    pe.wait_ge(A["qTc"], t * 2 - 1)
                    scores(0)
                for g in range(1, HEADS + 1):
                    if C_ and g < HEADS:
                        scores_t(g)
                    if B_ and 1 < g < 7:
                        if g == 3:
                            pe.wait_ge(A["qTc"], t * 2)
                        scores(g - 1)
                    if C_ and g == 1:
                        pe.wait_ge(A["vaug"], t - 1)
                        if D_:
                            pe.wait_ge(A["ow"], d + 1)
                    if A_ and g == 7:
                        pe.wait_ge(A["kcopy"], t + 1)
                        pe.wait_ge(A["vc"], t * 2 + 2)
                        turn8(k6, 0, bank[2][:]).then_inc(A["kTp"], 1)
                    if C_:
                        values(g - 1)
                    if A_ and g == 8:
                        if B_:
                            pe.wait_ge(A["smax"], b * 6 + 6)
                        turn8(q6, 0, bank[5][:]).then_inc(A["qTp"], 1)
                        turn8(k6, 1, bank[6][:]).then_inc(A["kTp"], 1)
                    if A_ and g == 1:
                        pe.wait_ge(A["xn"], t + 1)
                        for u in range(2):
                            last = pe.transpose(bank[1][:, u * P:u * P + P], axn[:, u, :], ident[:])
                        last.then_inc(A["xTp"], 1)
                    if A_ and g == 3:
                        pe.wait_ge(A["xTc"], t + 1)
                        for u in range(2):
                            pe.matmul(bank[1 + u][:, 0:3 * DIM], axT[:, u * P:u * P + P], wqkvo[:, 0:3, :], start=True, stop=True).then_inc(A["proj"], 1)
                    if D_ and g == 5:
                        if A_:
                            pe.wait_ge(A["vc"], t * 2 + 2)
                        pe.wait_ge(A["onorm"], d + 1)
                        for u in range(2):
                            last = pe.transpose(bank[1][:, u * P:u * P + P], od[:, u].rearrange("p a e -> p (a e)"), ident[:])
                        last.then_inc(A["oTp"], 1)
                    if D_ and g == 6:
                        pe.wait_ge(A["oTc"], d + 1)
                        for u in range(2):
                            last = pe.matmul(bank[1][:, (2 + u) * P:(3 + u) * P], oT[:, u * P:u * P + P], wqkvo[:, 3, :], start=True, stop=True)
                        last.then_inc(A["res"], 1)
            turns(pe, turn)

        def att_vector(dve, step):
            dve.wait_ge(s_ld_a, 80)
            step(dve.tensor_tensor(lam_p[:], lam_in[:, 0:4:2, :], lam_in[:, 1:4:2, :], ALU.mult))
            dve.tensor_reduce(lam_s[:], lam_p[:], X, ALU.add).then_inc(A["lam"], 1)
            dve.wait_ge(A["lame"], 1)
            step(dve.tensor_tensor(neg_lam[:], lam_e[:, 1:2], lam_e[:, 0:1], ALU.subtract))
            step(dve.tensor_scalar(neg_lam[:], neg_lam[:], -LAMBDA_INIT, None, ALU.add))
            dve.wait_ge(A["wTc"], 1)
            a_step, b_step, d_step = (LoopSteps(dve, A[n]) for n in ("astep", "bstep", "dstep"))

            def statistics(a):
                for u in range(2):
                    dve.bn_stats(ast[:, u, :], xs[:, bass.ds(a * 2 + u, 1), :]).then_inc(A["astep"], 1)
                    a_step.n += 1
                dve.wait_ge(A["astep"], a_step.base + a_step.n)
                dve.memset(hold[:, 0:1], 0.0)
                for u in range(2):
                    dve.bn_aggr(amv[:, u, :], ast[:, u, :]).then_inc(A["astep"], 1)
                    a_step.n += 1
                dve.wait_ge(A["astep"], a_step.base + a_step.n)
                dve.tensor_scalar(ave[:], amv[:, :, 1], EPS, None, ALU.add).then_inc(A["var"], 1)

            def norm(a):
                dve.wait_ge(A["rs"], a + 1)
                for u in range(2):
                    last = dve.tensor_scalar(axn[:, u, :], xs[:, bass.ds(a * 2 + u, 1), :].rearrange("p a e -> p (a e)"),
                                             amv[:, u, 0:1], ars[:, u:u + 1], ALU.subtract, ALU.mult)
                last.then_inc(A["xn"], 1)

            qk2 = qk[:].rearrange("p a u e -> p a (u e)")

            def split(a, j):
                if j == 0:
                    dve.wait_ge(A["qkv"], a * 2 + 2)
                    a_step(dve.tensor_scalar(qk2, qk2, GUARD, -GUARD, ALU.min, ALU.max))
                a_step(dve.tensor_copy(part[:, j], qk2))
                if j < 2:
                    a_step(dve.tensor_tensor(qk2, qk2, part[:, j], ALU.subtract))

            def pieces(a):
                if not (isinstance(a, int) and a == 0):
                    dve.wait_ge(A["qTc"], a * 2)
                for dst, w, j, at in ((k6, 1, 0, slice(0, 4, 3)), (k6, 1, 0, slice(5, 6)), (k6, 1, 1, slice(1, 5, 3)), (k6, 1, 2, slice(2, 3)),
                                      (q6, 0, 0, slice(0, 3)), (q6, 0, 1, slice(3, 5)), (q6, 0, 2, slice(5, 6))):
                    n = len(range(*at.indices(SLOTS)))
                    last = dve.tensor_copy(dst[:, :, at, :], part[:, j, w, :].rearrange("p (a e) -> p a e", e=HD)[:, :, None, :]
                                           .to_broadcast([P, 2 * SUB, n, HD]))
                last.then_inc(A["kcopy"], 1)

            def row_max(b, n):
                u, h0, per = (0, 8 * n, 4) if n < 2 else (1, 4 * (n - 2), 2)
                dve.wait_ge(A["s"], b * 6 + n + 1)
                c = u * SUB + h0
                dve.tensor_reduce(mx[:, c:c + 2 * per].rearrange("p (a q) -> p q a", q=2),
                                  quad[:, 2:4, :].rearrange("p q (a e) -> p q a e", a=per), X, ALU.max
                                  ).then_inc(A["smax"], 1)

            def max_parts(b):
                if not (isinstance(b, int) and b == 0):
                    dve.wait_ge(A["mTc"], b)
                dve.wait_ge(A["smax"], b * 6 + 6)
                b_step(dve.tensor_scalar(mx[:], mx[:], -1.0, None, ALU.mult))
                mxv = mx[:].rearrange("p (u g q) -> p u q g", u=2, q=2)
                mpv = mpart[:].rearrange("p u (q r) -> p u q r", q=2)
                for j in range(3):
                    pj = mpv[:, :, :, j:3 * HEADS:3]
                    if j < 2:
                        b_step(dve.tensor_copy(pj, mxv))
                        b_step(dve.tensor_tensor(mxv, mxv, pj, ALU.subtract))
                    else:
                        dve.tensor_copy(pj, mxv).then_inc(A["mparts"], 1)

            def weigh(d):
                dve.wait_ge(A["ot"], d + 1)
                obs = [bank[bk][:].rearrange("p (r e) -> p r e", e=32) for bk in (7, 0)]
                for u in range(2):
                    last = dve.reciprocal(rsum[:, u, :], obs[u][:, :, VD])
                d_step(last)
                second = rsum[:].rearrange("p u (j s g) -> p (u j) s g", s=2, g=4)[:, :, 1, :]
                d_step(dve.tensor_scalar(second, second, neg_lam[:], None, ALU.mult))
                for u in range(2):
                    last = dve.tensor_tensor(ow[:, u], obs[u][:, :, 0:VD], rsum[:, u, :, None].to_broadcast([P, SUB, VD]), ALU.mult)
                last.then_inc(A["ow"], 1)

            def outputs(d):
                dve.wait_ge(A["ow"], d + 1)
                owv = ow[:].rearrange("p u (j s g) e -> p (u j) s (g e)", s=2, g=4)
                d_step(dve.tensor_tensor(od[:].rearrange("p u (j g) e -> p (u j) (g e)", g=4), owv[:, :, 0, :], owv[:, :, 1, :], ALU.add))
                d_step(dve.tensor_tensor(osv, odv, odv, ALU.mult))
                d_step(dve.tensor_reduce(oms[:], osv, X, ALU.add))
                dve.tensor_scalar(oms[:], oms[:], 1.0 / VD, EPS, ALU.mult, ALU.add).then_inc(A["msq"], 1)

            odv = od[:].rearrange("p u a e -> p (u a) e")
            osv = osq[:].rearrange("p u a e -> p (u a) e")

            def rms(d):
                dve.wait_ge(A["rms"], d + 1)
                dve.tensor_tensor(odv, odv, orr[:, :, None].to_broadcast([P, 2 * HEADS, VD]), ALU.mult).then_inc(A["onorm"], 1)

            def residual(d):
                dve.wait_ge(A["res"], d + 1)
                x2 = xs[:, bass.ds(d * 2, 2), :]
                dve.tensor_tensor(x2, x2, bank[1][:, 2 * P:4 * P].rearrange("p (a e) -> p a e", e=DIM), ALU.add).then_inc(A["x2"], 1)

            def turn(t, par):
                A_, B_, C_, D_ = stages_of(t)
                b, d = t - 1, t - 3
                a_step.start(t * A_STEPS)
                b_step.start(b * B_STEPS)
                d_step.start(d * D_STEPS)
                if A_:
                    dve.wait_ge(sems["f1"]["comb"], t + 1)
                    statistics(t)
                if D_:
                    weigh(d)
                if A_:
                    norm(t)
                if B_:
                    dve.wait_ge(A["vc"], t * 2)
                    dve.tensor_copy(vaug[:, 1 - par, :, :, 0:VD], vnew[:].rearrange("p u (a e) -> p u a e", e=VD)).then_inc(A["vaug"], 1)
                if B_:
                    row_max(b, 0)
                if D_:
                    outputs(d)
                if B_:
                    row_max(b, 1)
                if D_:
                    rms(d)
                if B_:
                    row_max(b, 2)
                if A_:
                    split(t, 0)
                if B_:
                    row_max(b, 3)
                if A_:
                    split(t, 1)
                if B_:
                    row_max(b, 4)
                if A_:
                    split(t, 2)
                    pieces(t)
                if D_:
                    residual(d)
                if B_:
                    row_max(b, 5)
                    max_parts(b)
                if A_:
                    assert a_step.n == A_STEPS, a_step.n
                if B_:
                    assert b_step.n == B_STEPS, b_step.n
                if D_:
                    assert d_step.n == D_STEPS, d_step.n

            turns(dve, turn)
            dve.wait_ge(A["x2"], BATCH)

        def weights_vector(dve, step):
            dve.wait_ge(s_ld_w, 16 * 6)
            step(dve.tensor_copy(b1hi[:, 0, :], b1s[:]))
            step(dve.tensor_tensor(b1lo[:], b1s[:], b1hi[:, 0, :], ALU.subtract))
            step(dve.tensor_copy(b1hi[:, 1, :], b1lo[:]))
            step(dve.tensor_tensor(b1lo[:], b1lo[:], b1hi[:, 1, :], ALU.subtract))
            dve.tensor_copy(b1hi[:, 2, :], b1lo[:]).then_inc(s_b1, 1)
            w2cv = w2c[:].rearrange("p (a c d) -> p a c d", a=NE, c=FC)
            dve.wait_ge(s_b2m, 1)
            for h in range(2):
                step(dve.tensor_copy(b2p[:, 512 * h:512 * h + 512], bank[6 + h][:]))
            dve.sem_inc(s_b2c, 1)
            dve.wait_ge(s_w2g, 2)
            for h in range(2):
                dve.wait_ge(s_mean, h + 1)
                for a in range(4):
                    e = 4 * h + a
                    ins = dve.tensor_tensor(w2cv[:, e], w2cv[:, e],
                                            bank[1 + h][:, None, a * DIM:(a + 1) * DIM].to_broadcast([P, FC, DIM]), ALU.subtract)
                    if a < 3:
                        step(ins)
                ins.then_inc(s_w2c, 1)

        def weights_tensor(pe):
            pe.wait_ge(s_colc, 1)
            pe.wait_ge(s_ld_w2, 16)
            for h in range(2):
                for a in range(4):
                    e = 4 * h + a
                    o = bank[6 + h][:, a * DIM:(a + 1) * DIM]
                    for c in range(FC):
                        j = 32 + e * FC + c
                        pe.matmul(o, cols[:, j:j + 1].to_broadcast([P, P]), w2s[:, e, c, :], start=(c == 0), stop=False)
                    last = pe.matmul(o, ones[0:1, :], b2row[:, e * DIM:(e + 1) * DIM], start=False, stop=True)
            last.then_inc(s_b2m, 1)
            w2cv = w2c[:].rearrange("p (a c d) -> p a c d", a=NE, c=FC)
            for h in range(2):
                pe.wait_ge(s_w2g, h + 1)
                for c in range(FC):
                    last = pe.matmul(bank[1 + h][:].rearrange("p (a d) -> p a d", d=DIM), mean_w[:],
                                     w2cv[:, 4 * h:4 * h + 4, c, :], start=(c == 0), stop=(c == FC - 1))
                last.then_inc(s_mean, 1)

        b1s = sb("b1s", [32, P])
        hold = sb("hold", [1, 2])
        gpad = sb("gpad", [1, 2])

        @block.sync
        def _(sp):
            sp.dma_start(xs[:], x.rearrange("b (u p) d -> p (b u) d", p=P)).then_inc(s_ld_x, 16)
            sp.dma_start(wrs[:], Wr).then_inc(s_ld_w, 16)
            sp.dma_start(rows[0:32, :], g1.rearrange("a (c p) -> (a c) p", p=P)).then_inc(s_ld_w, 16)
            sp.dma_start(rows[32:64, :], be1.rearrange("a (c p) -> (a c) p", p=P)).then_inc(s_ld_w, 16)
            sp.dma_start(rows[64:96, :], b1.rearrange("a (c p) -> (a c) p", p=P)).then_inc(s_ld_w, 16)
            sp.dma_start(b1s[:], b1.rearrange("a (c p) -> (a c) p", p=P)).then_inc(s_ld_w, 16)
            sp.dma_start(b2row[:], b2.rearrange("(o a) d -> o (a d)", o=1)).then_inc(s_ld_w, 16)
            sp.dma_start(w2s[:].rearrange("p a c d -> p (a c) d"), W2.rearrange("a (c p) d -> p (a c) d", p=P)).then_inc(s_ld_w2, 16)
            sp.dma_start(w1s[:].rearrange("p (a f) -> p a f", a=NE), W1.rearrange("a p f -> p a f")).then_inc(s_ld_w1, 16)
            for j, w in enumerate((Wq, Wk, Wv, Wo)):
                sp.dma_start(wrow[:, j, :], w).then_inc(s_ld_a, 16)
            sp.wait_ge(s_b1, 1)
            for j in range(3):
                sp.dma_start(b1p[j:j + 1, :], b1hi[:, j, :]).then_inc(s_b1d, 16)
            for k in sems:
                moe_sync(sp, sems[k], k == list(sems)[-1])
            sp.wait_ge(s_out, 16 * BATCH)

        @block.gpsimd
        def _(pool):
            st = Steps(pool, s_pool)
            st(pool.memset(ones[:], 1.0))
            pool.affine_select(out=ident[:], in_=ones[:], compare_op=ALU.is_equal, fill=0.0, base=0,
                               pattern=[[-1, P]], channel_multiplier=1).then_inc(s_const, 1)
            pool.memset(mean_w[:], 1.0 / FF).then_inc(s_const, 1)
            pool.memset(eps_c[:], EPS).then_inc(s_const, 1)
            st(pool.memset(ones16[:], 1.0))
            pool.affine_select(out=before[:], in_=ones16[:], compare_op=ALU.is_gt, fill=0.0, base=0,
                               pattern=[[1, P]], channel_multiplier=-1).then_inc(s_const, 1)
            st(pool.memset(e_lt[:], 1.0))
            pool.affine_select(out=e_lt[:], in_=e_lt[:], compare_op=ALU.is_gt, fill=0.0, base=0,
                               pattern=[[1, NE], [-1, NE]], channel_multiplier=0).then_inc(s_const, 1)
            io = dict(channel_multiplier=0, allow_small_or_imprecise_dtypes=True)
            pool.iota(first_w[:], pattern=[[-1, NE]], base=NE, **io).then_inc(s_const, 1)
            pool.iota(lo_iota[:], pattern=[[1, P]], base=0, **io).then_inc(s_const, 1)
            pool.iota(tile_iota[:], pattern=[[1, 48]], base=0, **io).then_inc(s_const, 1)
            pool.iota(tcol[:], pattern=[[TT, TOPK], [1, TT]], base=0, **io).then_inc(s_const, 1)
            pool.iota(spare[:], pattern=[[P, 40]], base=1 + TOPK * TOK, channel_multiplier=1, allow_small_or_imprecise_dtypes=True).then_inc(s_const, 1)
            pool.iota(row_id[:], pattern=[[0, 1]], base=1, channel_multiplier=1, allow_small_or_imprecise_dtypes=True).then_inc(s_const, 1)
            pool.wait_ge(s_const, 11)
            st(pool.tensor_copy(ident16[:], ident[:]))
            st(pool.memset(mask_q[:], 0.0))
            pool.affine_select(out=mask_k[:], in_=mask_q[:], compare_op=ALU.is_ge, fill=-BIG, base=0,
                               pattern=[[1, P]], channel_multiplier=-1).then_inc(s_const, 1)
            pool.wait_ge(s_const, 12)
            pool.affine_select(out=mask_q[:], in_=mask_q[:], compare_op=ALU.is_ge, fill=-BIG, base=0,
                               pattern=[[-1, P]], channel_multiplier=1).then_inc(s_const, 1)
            pool.memset(neg_half[:], -0.5).then_inc(s_const, 1)
            st(pool.memset(q6[:].bitcast(F32), 0.0))
            st(pool.memset(k6[:].bitcast(F32), 0.0))
            st(pool.memset(mpart[:].bitcast(F32), 0.0))
            st(pool.memset(sel2[:], 1.0))
            st(pool.affine_select(out=sel2[:], in_=sel2[:], compare_op=ALU.is_ge, fill=0.0, base=0,
                                  pattern=[[-64, 2], [-3, HEADS]], channel_multiplier=1))
            st(pool.affine_select(out=sel2[:], in_=sel2[:], compare_op=ALU.is_ge, fill=0.0, base=2,
                                  pattern=[[64, 2], [3, HEADS]], channel_multiplier=-1))
            pool.tensor_tensor(sel[:], sel2[:, 0, :], sel2[:, 1, :], ALU.add).then_inc(s_const, 1)
            st(pool.memset(vaug[:], 0.0))
            pool.memset(vaug[:, :, :, :, VD:VD + 1], 1.0).then_inc(s_const, 1)
            pool.wait_ge(s_const, 16)
            pool.dma_start(brb[:], br.rearrange("(o a) -> o a", o=1).to_broadcast([P, NE])).then_inc(s_bc, 16)
            pool.dma_start(g2b[:], g2.rearrange("(o a) d -> o (a d)", o=1).to_broadcast([P, NE * DIM])).then_inc(s_bc, 16)
            pool.dma_start(be2b[:], be2.rearrange("(o a) d -> o (a d)", o=1).to_broadcast([P, NE * DIM])).then_inc(s_bc, 16)
            pool.wait_ge(s_bc, 48)
            pool.memset(gden[:], 0.0).then_inc(s_const, 1)
            pool.wait_ge(s_colc, 1)
            pool.wait_ge(s_ld_w2, 16)
            for h in range(2):
                pool.tensor_tensor(w2c[:].rearrange("p (a d) -> p a d", d=DIM)[:, 16 * h:16 * h + 16, :],
                                  w2s[:, 4 * h:4 * h + 4].rearrange("p a c d -> p (a c) d"),
                                  cols[:, 16 * h:16 * h + 16, None].to_broadcast([P, 16, DIM]), ALU.mult).then_inc(s_w2g, 1)
            for j, w in enumerate((lq1, lk1, lq2, lk2)):
                pool.dma_start(lam_in[:, j, :], w.rearrange("(o a) -> o a", o=1).to_broadcast([P, HD])).then_inc(s_lam, 16)
            pool.wait_ge(s_lam, 64)
            pool.memset(gpad[:, 0:1], 0.0).then_inc(s_ld_a, 16)
            moe_gpsimd(pool, sems["f1"])
            att_gpsimd(pool, sems["f1"])
            moe_gpsimd(pool, sems["f2"])

        @block.scalar
        def _(act):
            act.wait_ge(s_const, NCONST)
            for k in stages:
                att_scalar(act) if k == "at" else moe_scalar(act, sems[k])

        @block.tensor
        def _(pe):
            pe.wait_ge(s_ld_w, 16 * 6)
            pe.wait_ge(s_const, NCONST)
            pe.transpose(bank[6][:, 0:96], rows[:], ident[0:96, 0:96]).then_inc(s_cols, 1)
            for n, k in enumerate(stages):
                att_tensor(pe) if k == "at" else moe_tensor(pe, sems[k], n == 0)

        @block.vector
        def _(dve):
            step = Steps(dve, s_dve)
            dve.wait_ge(s_cols, 1)
            dve.tensor_copy(cols[:], bank[6][:, 0:96]).then_inc(s_colc, 1)
            moe_vector(dve, sems["f1"], step, True)
            att_vector(dve, step)
            moe_vector(dve, sems["f2"], step, False)
            for b in range(BATCH):
                combine_vector(dve, sems["f2"], b)


_INS = ['L0_attn_x', 'L0_attn_Wq', 'L0_attn_Wk', 'L0_attn_Wv', 'L0_attn_Wo', 'L0_attn_lq1', 'L0_attn_lk1',
        'L0_attn_lq2', 'L0_attn_lk2', 'L0_ffn_Wr', 'L0_ffn_br', 'L0_ffn_W1', 'L0_ffn_b1', 'L0_ffn_g1',
        'L0_ffn_be1', 'L0_ffn_W2', 'L0_ffn_b2', 'L0_ffn_g2', 'L0_ffn_be2']
STAGES = ("f1", "at", "f2")


def kernel(**inputs):
    import numpy as _np
    import concourse.bacc as _bacc
    from concourse import mybir as _mybir
    from concourse.bass_utils import run_bass_kernel_spmd as _run

    nc = _bacc.Bacc("TRN2", target_bir_lowering=False, num_devices=1)
    arrays, args = {}, []
    for name in _INS:
        a = _np.ascontiguousarray(inputs[name])
        arrays[f"in_{name}_dram"] = a
        args.append(nc.dram_tensor(f"in_{name}_dram", a.shape, _mybir.dt.from_np(a.dtype), kind="ExternalInput").ap())
    args.append(nc.dram_tensor("out_0_dram", (BATCH, SEQ, DIM), F32, kind="ExternalOutput").ap())
    build(nc, *args, stages=STAGES)
    r = _run(nc, [arrays], core_ids=[0])
    return r.results[0]["out_0_dram"]
```
